# Optimizing a Trainium2 kernel written in Bass

```python
import numpy as np
import jax
import jax.numpy as jnp

def _softmax(x, axis=-1):
    return jax.nn.softmax(x, axis=axis)

def _gelu(x):
    return jax.nn.gelu(x, approximate=True)

def _silu(x):
    return jax.nn.silu(x)

def _sigmoid(x):
    return jax.nn.sigmoid(x)

def _layernorm(x, axis=-1, eps=1e-05):
    m = jnp.mean(x, axis=axis, keepdims=True)
    v = jnp.var(x, axis=axis, keepdims=True)
    return (x - m) / jnp.sqrt(v + eps)

def _scatter_add(tgt, idx, src, axis=0):
    return tgt.at[idx].add(src)

def _segment_sum(src, seg, n):
    return jax.ops.segment_sum(src, seg, n)
kernel_name = 'mk_decoder_preln_d1_seqx_r4_c69451'

def setup_inputs(seed: int=0):
    np.random.seed(seed)
    _w = jnp.asarray

    def _rec_inputs():
        import jax
        import jax.numpy as jnp
        _rk = jax.random.key(seed)
        x = -0.0002928 + 1 * jax.random.normal(jax.random.fold_in(_rk, 1), (128, 128, 256), jnp.float32)
        _lenS = 128 - jax.random.randint(jax.random.fold_in(_rk, 7), (128,), 0, max(1, 128 // 4) + 1, jnp.int32)
        _lenS2 = 128 - jax.random.randint(jax.random.fold_in(_rk, 8), (128,), 0, max(1, 128 // 4) + 1, jnp.int32)
        _ctx_1024P = jax.random.normal(jax.random.fold_in(_rk, 11), (128, 16, 256), jnp.float32)
        _ctx_1024c = jax.random.dirichlet(jax.random.fold_in(_rk, 511), 0.3 * jnp.ones((16,), jnp.float32), (128, 128))
        _ctx_1024t = jnp.einsum('bsk,bkd->bsd', _ctx_1024c, _ctx_1024P)
        _ctx_1024t = _ctx_1024t * jax.lax.rsqrt(jnp.mean(jnp.square(_ctx_1024t)) + 1e-12) * 0.953939
        ctx_1024 = -1.39393e-06 + 0.999914 * (_ctx_1024t + 0.3 * jax.random.normal(jax.random.fold_in(_rk, 611), (128, 128, 256), jnp.float32))
        _validS = jnp.arange(128)[None, :] < _lenS[:, None]
        _validS2 = jnp.arange(128)[None, :] < _lenS2[:, None]
        _causal = jnp.tril(jnp.ones((128, 128), dtype=bool))
        mask_1x1xSxS2_ik1 = jnp.where(jnp.broadcast_to(_validS2[0:1, None, None, :], (1, 1, 128, 128)), 1, 0).astype(jnp.int32)
        return (x, ctx_1024, mask_1x1xSxS2_ik1)
    x, ctx_1024, mask_1x1xSxS2_ik1 = _rec_inputs()

    def _L0_attn_setup():
        import jax, jax.numpy as jnp
        import numpy as np
        HEAD_NUM = 16
        key = jax.random.key(seed)
        ks = jax.random.split(key, 9)
        B, S, D = (4, 512, 256)

        def xavier(k, shape):
            limit = jnp.sqrt(6.0 / (shape[0] + shape[1]))
            return jax.random.uniform(k, shape, jnp.float32, -limit, limit)
        return {'x': jax.random.normal(ks[0], (B, S, D), jnp.float32), 'Wq': xavier(ks[1], (D, D)), 'bq': jnp.zeros((D,), jnp.float32), 'Wk': xavier(ks[2], (D, D)), 'bk': jnp.zeros((D,), jnp.float32), 'Wv': xavier(ks[3], (D, D)), 'bv': jnp.zeros((D,), jnp.float32), 'Wo': xavier(ks[4], (D, D)), 'bo': jnp.zeros((D,), jnp.float32)}
    _L0_attn_all = _L0_attn_setup()
    _L0_attn_in = {k: v for k, v in _L0_attn_all.items() if k in ('Wq', 'bq', 'Wk', 'bk', 'Wv', 'bv', 'Wo', 'bo')}
    del _L0_attn_all

    def _L0_xattn_setup():
        import jax, jax.numpy as jnp
        import numpy as np
        D_MODEL = 256
        H = 16
        D_K = D_MODEL // H
        key = jax.random.key(seed)
        ks = jax.random.split(key, 12)
        B, S = (2, 512)
        inp = {'q': jax.random.normal(ks[0], (B, S, D_MODEL), jnp.float32), 'k': jax.random.normal(ks[1], (B, S, D_MODEL), jnp.float32), 'v': jax.random.normal(ks[2], (B, S, D_MODEL), jnp.float32), 'mask': jax.random.randint(ks[3], (1, 1, S, S), 0, 2, jnp.int32)}
        s = 1.0 / np.sqrt(D_MODEL)
        inp['wq_w'] = jax.random.normal(ks[4], (D_MODEL, D_MODEL), jnp.float32) * s
        inp['wq_b'] = jnp.zeros((D_MODEL,), jnp.float32)
        inp['wk_w'] = jax.random.normal(ks[5], (D_MODEL, D_MODEL), jnp.float32) * s
        inp['wk_b'] = jnp.zeros((D_MODEL,), jnp.float32)
        inp['wv_w'] = jax.random.normal(ks[6], (D_MODEL, D_MODEL), jnp.float32) * s
        inp['wv_b'] = jnp.zeros((D_MODEL,), jnp.float32)
        inp['wo_w'] = jax.random.normal(ks[7], (D_MODEL, D_MODEL), jnp.float32) * s
        inp['wo_b'] = jnp.zeros((D_MODEL,), jnp.float32)
        return inp
    _L0_xattn_all = _L0_xattn_setup()
    _L0_xattn_in = {k: v for k, v in _L0_xattn_all.items() if k in ('wq_w', 'wq_b', 'wk_w', 'wk_b', 'wv_w', 'wv_b', 'wo_w', 'wo_b')}
    del _L0_xattn_all

    def _L0_ffn_setup():
        import jax, jax.numpy as jnp
        import numpy as np
        EPS = 1e-06
        LN_EPS = 1e-05

        def _absmean_core(W):
            gamma = jnp.mean(jnp.abs(W)) + EPS
            Ws = W / gamma
            Wq = jnp.sign(Ws) * jnp.minimum(jnp.round(jnp.abs(Ws)), 1.0)
            return (Wq, gamma)

        @jax.custom_vjp
        def absmean(W):
            return _absmean_core(W)[0]

        def _absmean_fwd(W):
            Wq, gamma = _absmean_core(W)
            return (Wq, gamma)

        def _absmean_bwd(gamma, g):
            return (g / gamma,)
        absmean.defvjp(_absmean_fwd, _absmean_bwd)

        def layernorm(x, w, b, eps=LN_EPS):
            mu = jnp.mean(x, axis=-1, keepdims=True)
            var = jnp.mean((x - mu) ** 2, axis=-1, keepdims=True)
            return (x - mu) * jax.lax.rsqrt(var + eps) * w + b
        key = jax.random.key(seed)
        k1, k2, k3 = jax.random.split(key, 3)
        d, h = (256, 1024)
        B, T = (8, 512)
        return {'x': jax.random.normal(k1, (B, T, d), jnp.float32), 'W_fc': jax.random.normal(k2, (h, d), jnp.float32), 'ln_w': jnp.ones((h,), jnp.float32), 'ln_b': jnp.zeros((h,), jnp.float32), 'W_proj': jax.random.normal(k3, (d, h), jnp.float32)}
    _L0_ffn_all = _L0_ffn_setup()
    _L0_ffn_in = {k: v for k, v in _L0_ffn_all.items() if k in ('W_fc', 'ln_w', 'ln_b', 'W_proj')}
    del _L0_ffn_all
    return {'x': x, 'ctx_1024': ctx_1024, 'mask_1x1xSxS2_ik1': mask_1x1xSxS2_ik1, 'L0_attn_Wq': _L0_attn_in['Wq'], 'L0_attn_bq': _L0_attn_in['bq'], 'L0_attn_Wk': _L0_attn_in['Wk'], 'L0_attn_bk': _L0_attn_in['bk'], 'L0_attn_Wv': _L0_attn_in['Wv'], 'L0_attn_bv': _L0_attn_in['bv'], 'L0_attn_Wo': _L0_attn_in['Wo'], 'L0_attn_bo': _L0_attn_in['bo'], 'L0_xattn_wq_w': _L0_xattn_in['wq_w'], 'L0_xattn_wq_b': _L0_xattn_in['wq_b'], 'L0_xattn_wk_w': _L0_xattn_in['wk_w'], 'L0_xattn_wk_b': _L0_xattn_in['wk_b'], 'L0_xattn_wv_w': _L0_xattn_in['wv_w'], 'L0_xattn_wv_b': _L0_xattn_in['wv_b'], 'L0_xattn_wo_w': _L0_xattn_in['wo_w'], 'L0_xattn_wo_b': _L0_xattn_in['wo_b'], 'L0_ffn_W_fc': _L0_ffn_in['W_fc'], 'L0_ffn_ln_w': _L0_ffn_in['ln_w'], 'L0_ffn_ln_b': _L0_ffn_in['ln_b'], 'L0_ffn_W_proj': _L0_ffn_in['W_proj']}

def reference(x, ctx_1024, mask_1x1xSxS2_ik1, L0_attn_Wq, L0_attn_bq, L0_attn_Wk, L0_attn_bk, L0_attn_Wv, L0_attn_bv, L0_attn_Wo, L0_attn_bo, L0_xattn_wq_w, L0_xattn_wq_b, L0_xattn_wk_w, L0_xattn_wk_b, L0_xattn_wv_w, L0_xattn_wv_b, L0_xattn_wo_w, L0_xattn_wo_b, L0_ffn_W_fc, L0_ffn_ln_w, L0_ffn_ln_b, L0_ffn_W_proj):
    import jax
    import jax.numpy as jnp

    def _L0_attn_ref(x, Wq, bq, Wk, bk, Wv, bv, Wo, bo):
        import jax, jax.numpy as jnp
        import numpy as np
        HEAD_NUM = 16
        B, S, D = x.shape
        H = HEAD_NUM
        hd = D // H

        def proj(W, b):
            return (x @ W.T + b).reshape(B, S, H, hd).transpose(0, 2, 1, 3)
        Q, K, V = (proj(Wq, bq), proj(Wk, bk), proj(Wv, bv))
        scale = 1.0 / jnp.sqrt(jnp.float32(hd))
        scores = jnp.einsum('bhqd,bhkd->bhqk', Q, K) * scale
        attn = jax.nn.softmax(scores, axis=-1)
        out = jnp.einsum('bhqk,bhkd->bhqd', attn, V)
        out = out.transpose(0, 2, 1, 3).reshape(B, S, D)
        return out @ Wo.T + bo

    def _L0_xattn_ref(q, k, v, mask, wq_w, wq_b, wk_w, wk_b, wv_w, wv_b, wo_w, wo_b):
        import jax, jax.numpy as jnp
        import numpy as np
        D_MODEL = 256
        H = 16
        D_K = D_MODEL // H
        B, S, _ = q.shape

        def proj(x, w, b):
            y = x @ w.T + b
            return y.reshape(B, S, H, D_K).transpose(0, 2, 1, 3)
        Q = proj(q, wq_w, wq_b)
        K = proj(k, wk_w, wk_b)
        V = proj(v, wv_w, wv_b)
        scores = jnp.einsum('bhqd,bhkd->bhqk', Q, K) / jnp.sqrt(jnp.float32(D_K))
        scores = jnp.where(mask == 0, jnp.float32(1e-09), scores)
        attn = jax.nn.softmax(scores, axis=-1)
        out = jnp.einsum('bhqk,bhkd->bhqd', attn, V)
        out = out.transpose(0, 2, 1, 3).reshape(B, S, H * D_K)
        return out @ wo_w.T + wo_b

    def _L0_ffn_ref(x, W_fc, ln_w, ln_b, W_proj):
        import jax, jax.numpy as jnp
        import numpy as np
        EPS = 1e-06
        LN_EPS = 1e-05

        def _absmean_core(W):
            gamma = jnp.mean(jnp.abs(W)) + EPS
            Ws = W / gamma
            Wq = jnp.sign(Ws) * jnp.minimum(jnp.round(jnp.abs(Ws)), 1.0)
            return (Wq, gamma)

        @jax.custom_vjp
        def absmean(W):
            return _absmean_core(W)[0]

        def _absmean_fwd(W):
            Wq, gamma = _absmean_core(W)
            return (Wq, gamma)

        def _absmean_bwd(gamma, g):
            return (g / gamma,)
        absmean.defvjp(_absmean_fwd, _absmean_bwd)

        def layernorm(x, w, b, eps=LN_EPS):
            mu = jnp.mean(x, axis=-1, keepdims=True)
            var = jnp.mean((x - mu) ** 2, axis=-1, keepdims=True)
            return (x - mu) * jax.lax.rsqrt(var + eps) * w + b
        h = jnp.einsum('btd,hd->bth', x, absmean(W_fc))
        h = jax.nn.gelu(h, approximate=False)
        h = layernorm(h, ln_w, ln_b)
        return jnp.einsum('bth,dh->btd', h, absmean(W_proj))
    x = x + _L0_attn_ref(_layernorm(x, axis=-1), L0_attn_Wq, L0_attn_bq, L0_attn_Wk, L0_attn_bk, L0_attn_Wv, L0_attn_bv, L0_attn_Wo, L0_attn_bo)
    x = x + _L0_xattn_ref(_layernorm(x, axis=-1), ctx_1024, ctx_1024, mask_1x1xSxS2_ik1, L0_xattn_wq_w, L0_xattn_wq_b, L0_xattn_wk_w, L0_xattn_wk_b, L0_xattn_wv_w, L0_xattn_wv_b, L0_xattn_wo_w, L0_xattn_wo_b)
    x = x + _L0_ffn_ref(_layernorm(x, axis=-1), L0_ffn_W_fc, L0_ffn_ln_w, L0_ffn_ln_b, L0_ffn_W_proj)
    return x

_drawn_inputs = setup_inputs


def setup_inputs(seed=0):
    import zlib

    import numpy as np

    out = dict(_drawn_inputs(seed))
    spreads = {'L0_attn_bq': (0.0, 0.532),
     'L0_attn_bk': (0.0, 0.8),
     'L0_attn_bv': (0.0, 0.1),
     'L0_attn_bo': (0.0, 0.1),
     'L0_xattn_wq_b': (0.0, 0.344),
     'L0_xattn_wk_b': (0.0, 0.8),
     'L0_xattn_wv_b': (0.0, 0.1),
     'L0_xattn_wo_b': (0.0, 0.1),
     'L0_ffn_ln_w': (1.0, 0.2),
     'L0_ffn_ln_b': (0.0, 0.1)}
    factors = {}
    for name, (base, spread) in spreads.items():
        noise = np.random.default_rng([zlib.crc32(name.encode()), seed]).standard_normal(out[name].shape)
        drawn = base * np.exp(spread * noise) if base else spread * noise
        out[name] = jnp.asarray(drawn.astype(out[name].dtype))
    for name, factor in factors.items():
        out[name] = (out[name] * factor).astype(out[name].dtype)
    return out
```

```python
from contextlib import ExitStack

import concourse.bass as bass
from concourse import mybir

F32, F16, BF16, I32 = mybir.dt.float32, mybir.dt.float16, mybir.dt.bfloat16, mybir.dt.int32
ALU = mybir.AluOpType
ACT = mybir.ActivationFunctionType
AX = mybir.AxisListType

P = 128
B, S, D = 128, 128, 256
H = 16
HD = D // H
F = 1024
G = 4
NG = B // G
T = G * S
KT = D // P
FT = F // P
PAIRS = H // 2
HALF = 64
STACK = 3 * HD
QUADS = H // 4
VW = 32
WS = 8.0
SHIFT = WS * WS
EXP_SCALE = 1.0 / (HD ** 0.5 * SHIFT)
LN_EPS = 1e-5
GAMMA_EPS = 1e-6
MASKED = 1e-9
NEG = -1e30
HI, LO = 0, 1
SPLITS = ((HI, HI), (LO, HI), (HI, LO))

SQ, SK, SV, SO, XQ, XK, XV, XO = range(8)
STACK_DMAS = 4 * FT


class Inputs:

    def __init__(self, x, ctx, mask, sWq, sbq, sWk, sbk, sWv, sbv, sWo, sbo,
                 xWq, xbq, xWk, xbk, xWv, xbv, xWo, xbo, Wfc, lnw, lnb, Wp):
        self.x, self.ctx, self.mask = x, ctx, mask
        self.weights = [sWq, sWk, sWv, sWo, xWq, xWk, xWv, xWo]
        self.qk_biases = [sbq, sbk, xbq, xbk]
        self.v_biases, self.o_biases = [sbv, xbv], [sbo, xbo]
        self.Wfc, self.lnw, self.lnb, self.Wp = Wfc, lnw, lnb, Wp


class Shared:

    def __init__(self, sb):
        self.WT = sb("WT", [P, 8, 2, KT, D], F16)
        self.wfcT = sb("wfcT", [P, KT, F], F16)
        self.wpT = sb("wpT", [P, FT, D], F16)
        self.bcol = sb("bcol", [P, 4, KT])
        self.bv2 = sb("bv2", [P, 2, 2, D])
        self.boB = sb("boB", [P, 2, D])
        self.lnwB = sb("lnwB", [P, F])
        self.c2B = sb("c2B", [P, D])
        self.ident = sb("ident", [P, P])
        self.ident16 = sb("ident16", [P, P], F16)
        self.identb = sb("identb", [P, P], BF16)
        self.mhalf = sb("mhalf", [P, G])
        self.maskB4 = sb("maskB4", [P, 4, S], BF16)
        self.maskBT4 = sb("maskBT4", [P, G, S], BF16)
        self.maskcT = sb("maskcT", [P, S])
        self.cntW = sb("cntW", [P, 1])
        self.mfloor = sb("mfloor", [P, 1])


def allocators(nc, stack, program):
    sb = lambda name, shape, dt=F32: stack.enter_context(nc.sbuf_tensor(name, shape, dt))
    ps = lambda name, shape, dt=F32: stack.enter_context(nc.psum_tensor(name, shape, dt))
    sem = lambda name: program.enter_context(nc.semaphore(name))
    return sb, ps, sem


def wait(engine, sem, count):
    if not isinstance(count, int) or count > 0:
        engine.wait_ge(sem, count)


def decoder_layer_kernel(nc, ins, out):
    x2_dram = nc.dram_tensor("x2_scratch", (B, S, D), F32, kind="Internal").ap()
    with ExitStack() as stack:
        sb, _, _ = allocators(nc, stack, stack)
        sh = Shared(sb)
        setup(nc, stack, ins, sh)
        attention(nc, stack, ins, sh, x2_dram)
        ffn(nc, stack, sh, x2_dram, out)


def setup(nc, program, ins, sh):
    WT, wfcT, wpT, bcol, bv2, boB, lnwB, c2B = sh.WT, sh.wfcT, sh.wpT, sh.bcol, sh.bv2, sh.boB, sh.lnwB, sh.c2B
    ident, ident16, identb, mhalf = sh.ident, sh.ident16, sh.identb, sh.mhalf
    maskB4, maskBT4, maskcT, cntW, mfloor = sh.maskB4, sh.maskBT4, sh.maskcT, sh.cntW, sh.mfloor

    with ExitStack() as stack:
        sb, ps, sem = allocators(nc, stack, program)
        wnat = sb("wnat", [P, 8, KT, D])
        fnat = sb("fnat", [P, 2, F * KT])
        neg = sb("neg", [P, 2, F * KT])
        junk = sb("junk", [P, F * KT])
        wpT32 = sb("wpT32", [P, FT, D])
        lnb_col = sb("lnb_col", [P, FT])
        lnbB = sb("lnbB", [P, FT, P])
        ones = sb("ones", [P, P])
        asum = sb("asum", [P, 2])
        thr = sb("thr", [P, 2])
        nthr = sb("nthr", [P, 2])
        imask = sb("imask", [P, S], I32)
        maskc = sb("maskc", [P, S])
        bank = ps("setup_bank", [P, 8, 512])

        w_in = sem("w_in")
        f_in, small_in, mask_in = sem("f_in"), sem("small_in"), sem("mask_in")
        zeroed, consts = sem("zeroed"), sem("consts")
        w_T, w_hi, w_lo = sem("w_T"), sem("w_hi"), sem("w_lo")
        abs_done, total_done, gamma_done, thr_done = sem("abs_done"), sem("total_done"), sem("gamma_done"), sem("thr_done")
        neg_done, tern_done, f_T, f_out = sem("neg_done"), sem("tern_done"), sem("f_T"), sem("f_out")
        lnb_done, c2_mm, c2_done = sem("lnb_done"), sem("c2_mm"), sem("c2_done")
        m_done, mc_done, m_T, m_out, cnt_done = sem("m_done"), sem("mc_done"), sem("m_T"), sem("m_out"), sem("cnt_done")
        scaled = sem("scaled")
        NSMALL = 4 + 4 + 2 + 1 + 1

        with nc.Block() as block:
            @block.sync
            def _(sp):
                for n, w in enumerate(ins.weights):
                    sp.dma_start(wnat[:, n], w.rearrange("(m p) i -> p m i", p=P)).then_inc(w_in, 16)
                for n, b in enumerate(ins.qk_biases):
                    sp.dma_start(bcol[:, n], b.rearrange("(m p) -> p m", p=P), allow_slow_non_contiguous=True).then_inc(small_in, 16)
                sp.dma_start(lnb_col[:, :], ins.lnb.rearrange("(t p) -> p t", p=P), allow_slow_non_contiguous=True).then_inc(small_in, 16)

            @block.scalar
            def _(act):
                act.dma_start(fnat[:, 0], ins.Wfc.rearrange("(t p) d -> p t d", p=P)).then_inc(f_in, 16)
                act.dma_start(fnat[:, 1], ins.Wp.rearrange("(t p) h -> p t h", p=P)).then_inc(f_in, 16)
                act.dma_start(imask[:, :], ins.mask[0, 0]).then_inc(mask_in, 16)
                for n in range(2):
                    for twice in range(2):
                        act.dma_start(bv2[:, n, twice], ins.v_biases[n].partition_broadcast(P)).then_inc(small_in, 16)
                    act.dma_start(boB[:, n], ins.o_biases[n].partition_broadcast(P)).then_inc(small_in, 16)
                act.dma_start(lnwB[:, :], ins.lnw.partition_broadcast(P)).then_inc(small_in, 16)
                act.wait_ge(f_in, 32)
                for n in range(2):
                    if n:
                        act.wait_ge(abs_done, n)
                    nc.scalar.activation(junk[:, :], fnat[:, n], ACT.Abs, accum_out=asum[:, n:n + 1]).then_inc(abs_done, 1)
                for n in range(8):
                    act.wait_ge(w_T, n + 1)
                    nc.scalar.activation(WT[:, n, HI], bank[:, n, :].rearrange("p (k o) -> p k o", k=KT),
                                         ACT.Copy, scale=WS).then_inc(w_hi, 1)

            @block.gpsimd
            def _(pool):
                for t in (ident, ident16, identb):
                    nc.gpsimd.memset(t[:, :], 0.0).then_inc(zeroed, 1)
                nc.gpsimd.memset(ones[:, :], 1.0).then_inc(zeroed, 1)
                nc.gpsimd.memset(mhalf[:, :], -0.5).then_inc(zeroed, 1)
                pool.wait_ge(zeroed, 5)
                for t in (ident, ident16, identb):
                    nc.gpsimd.affine_select(out=t[:, :], in_=t[:, :], compare_op=ALU.not_equal, fill=1.0,
                                            base=0, pattern=[[-1, P]], channel_multiplier=1).then_inc(consts, 1)

            @block.vector
            def _(dve):
                dve.wait_ge(total_done, 1)
                nc.vector.tensor_scalar(thr[:, :], bank[:, 7, 0:2], 1.0 / (F * D), GAMMA_EPS, ALU.mult, ALU.add).then_inc(gamma_done, 1)
                dve.wait_ge(gamma_done, 1)
                nc.vector.tensor_scalar(nthr[:, :], thr[:, :], -0.5, None, ALU.mult).then_inc(thr_done, 1)
                dve.wait_ge(thr_done, 1)
                nc.vector.tensor_scalar(thr[:, :], thr[:, :], 0.5, None, ALU.mult).then_inc(thr_done, 1)
                dve.wait_ge(thr_done, 2)
                for n in range(2):
                    nc.vector.tensor_scalar(neg[:, n], fnat[:, n], nthr[:, n:n + 1], None, ALU.is_lt).then_inc(neg_done, 1)
                for n in range(2):
                    dve.wait_ge(neg_done, n + 1)
                    nc.vector.scalar_tensor_tensor(fnat[:, n], fnat[:, n], thr[:, n:n + 1], neg[:, n],
                                                   ALU.is_gt, ALU.subtract).then_inc(tern_done, 1)
                for n in range(8):
                    dve.wait_ge(w_hi, n + 1)
                    nc.vector.scalar_tensor_tensor(WT[:, n, LO].rearrange("p k o -> p (k o)"), bank[:, n, :], WS,
                                                   WT[:, n, HI].rearrange("p k o -> p (k o)"),
                                                   ALU.mult, ALU.subtract).then_inc(w_lo, 1)
                dve.wait_ge(small_in, 16 * NSMALL)
                nc.vector.tensor_scalar(bcol[:, :, :], bcol[:, :, :], WS, None, ALU.mult).then_inc(scaled, 1)
                nc.vector.tensor_scalar(bv2[:, :, :, :], bv2[:, :, :, :], WS, None, ALU.mult).then_inc(scaled, 1)
                for t in range(FT):
                    last = nc.vector.tensor_copy(lnbB[:, t], lnb_col[:, t:t + 1].broadcast_to([P, P]))
                last.then_inc(lnb_done, 1)
                for kt in range(KT):
                    dve.wait_ge(f_T, kt + 1)
                    nc.vector.tensor_copy(wfcT[:, kt].rearrange("p (a h) -> p a h", a=2), bank[:, 2 * kt:2 * kt + 2, :]).then_inc(f_out, 1)
                dve.wait_ge(f_T, KT + 1)
                nc.vector.tensor_copy(wpT[:, :, :].rearrange("p (a t) d -> p a (t d)", a=4), bank[:, 4:8, :]).then_inc(f_out, 1)
                nc.vector.tensor_copy(wpT32[:, :, :].rearrange("p (a t) d -> p a (t d)", a=4), bank[:, 4:8, :]).then_inc(f_out, 1)
                dve.wait_ge(c2_mm, 1)
                nc.vector.tensor_copy(c2B[:, :], bank[:, 0, 0:D]).then_inc(c2_done, 1)
                dve.wait_ge(mask_in, 16)
                nc.vector.tensor_copy(maskc[:, :], imask[:, :]).then_inc(m_done, 1)
                dve.wait_ge(m_done, 1)
                nc.vector.tensor_scalar(maskc[:, :], maskc[:, :], 0.0, None, ALU.is_equal).then_inc(mc_done, 1)
                dve.wait_ge(mc_done, 1)
                nc.vector.tensor_reduce(cntW[:, :], maskc[:, :], AX.X, ALU.add).then_inc(cnt_done, 1)
                for n in range(4):
                    nc.vector.tensor_scalar(maskB4[:, n], maskc[:, :], NEG, None, ALU.mult)
                dve.wait_ge(cnt_done, 1)
                nc.vector.tensor_scalar(mfloor[:, :], cntW[:, :], 0.0, NEG, ALU.is_le, ALU.mult).then_inc(cnt_done, 1)
                dve.wait_ge(cnt_done, 2)
                nc.vector.tensor_scalar(mfloor[:, :], mfloor[:, :], MASKED * HD ** 0.5 * SHIFT, None, ALU.add).then_inc(cnt_done, 1)
                nc.vector.tensor_scalar(cntW[:, :], cntW[:, :], WS, None, ALU.mult).then_inc(cnt_done, 1)
                dve.wait_ge(m_T, 1)
                nc.vector.tensor_copy(maskcT[:, :], bank[:, 1, 0:S]).then_inc(m_out, 1)
                for n in range(G):
                    nc.vector.tensor_scalar(maskBT4[:, n], bank[:, 1, 0:S], NEG, None, ALU.mult).then_inc(m_out, 1)

            @block.tensor
            def _(pe):
                pe.wait_ge(consts, 3)
                pe.wait_ge(abs_done, 2)
                nc.tensor.matmul(bank[:, 7, 0:2], ones[:, :], asum[:, :], start=True, stop=True).then_inc(total_done, 1)
                pe.wait_ge(gamma_done, 1)
                pe.wait_ge(w_in, 16 * 8)
                for n in range(8):
                    for mt in range(KT):
                        for kt in range(KT):
                            last = nc.tensor.transpose(bank[:, n, kt * D + mt * P:kt * D + (mt + 1) * P],
                                                       wnat[:, n, mt, kt * P:(kt + 1) * P], ident[:, :])
                    last.then_inc(w_T, 1)
                pe.wait_ge(w_lo, 8)
                pe.wait_ge(tern_done, 2)
                fc = fnat[:, 0].rearrange("p (t d) -> p t d", t=FT)
                pj = fnat[:, 1].rearrange("p (t h) -> p t h", t=KT)
                for kt in range(KT):
                    for t in range(FT):
                        last = nc.tensor.transpose(bank[:, 2 * kt + t // 4, (t % 4) * P:(t % 4 + 1) * P],
                                                   fc[:, t, kt * P:(kt + 1) * P], ident[:, :])
                    last.then_inc(f_T, 1)
                for t in range(FT):
                    for m in range(KT):
                        o = (t % 2) * D + m * P
                        last = nc.tensor.transpose(bank[:, 4 + t // 2, o:o + P], pj[:, m, t * P:(t + 1) * P], ident[:, :])
                last.then_inc(f_T, 1)
                pe.wait_ge(f_out, 4)
                pe.wait_ge(lnb_done, 1)
                for t in range(FT):
                    last = nc.tensor.matmul(bank[:, 0, 0:D], lnbB[:, t], wpT32[:, t], start=(t == 0), stop=(t == FT - 1))
                last.then_inc(c2_mm, 1)
                pe.wait_ge(mc_done, 1)
                nc.tensor.transpose(bank[:, 1, 0:S], maskc[:, :], ident[:, :]).then_inc(m_T, 1)


class Chain:

    def __init__(self, name, sb, ps, sem, first_weight):
        n = name
        self.cross = name == "cross"
        self.wq, self.wk, self.wv, self.wo = range(first_weight, first_weight + 4)
        self.which = 1 if self.cross else 0
        self.src = sb(n + "_src", [P, G, D])
        self.stats = sb(n + "_stats", [P, G, 6])
        self.mv = sb(n + "_mv", [P, G, 2])
        self.ve = sb(n + "_ve", [P, G])
        self.rstd = sb(n + "_rstd", [P, G])
        self.xn = sb(n + "_xn", [P, G, D])
        self.xb = sb(n + "_xb", [P, G, D])
        self.xhl = sb(n + "_xhl", [P, 2, KT, T], F16)
        self.qk = sb(n + "_qk", [P, 4, KT, T], F16)
        self.stk = sb(n + "_stk", [P, 2, PAIRS, T], F16)
        self.vals = sb(n + "_vals", [P, G, H, VW])
        self.prob = sb(n + "_prob", [P, 2, 4, T])
        self.oT = self.qk[:, :, :, :].rearrange("p a k t -> p (a k t)").bitcast(F32).rearrange("p (q t) -> p q t", q=QUADS)
        self.mx = sb(n + "_mx", [P, G * H])
        self.negm = sb(n + "_negm", [P, G * H], F16)
        self.negmT = sb(n + "_negmT", [H, T], F16)
        self.rec = sb(n + "_rec", [P, QUADS, G * 4])
        self.bk = ps(n + "_bk", [P, 4, 512])
        if not self.cross:
            self.loaded = sem("self_loaded")
        self.stats_done = sem(n + "_stats_done")
        self.moments = sem(n + "_moments")
        self.var_ready = sem(n + "_var_ready")
        self.rstd_ready = sem(n + "_rstd_ready")
        self.xn_ready = sem(n + "_xn_ready")
        self.xb_ready = sem(n + "_xb_ready")
        self.xT_ready = sem(n + "_xT_ready")
        self.xhi_ready = sem(n + "_xhi_ready")
        self.xlo_ready = sem(n + "_xlo_ready")
        self.qk_mm = sem(n + "_qk_mm")
        self.qk_hi = sem(n + "_qk_hi")
        self.qk_lo = sem(n + "_qk_lo")
        self.v_mm = sem(n + "_v_mm")
        self.v_ready = sem(n + "_v_ready")
        self.stacked = sem(n + "_stacked")
        self.s_mm = sem(n + "_s_mm")
        self.max_done = sem(n + "_max_done")
        self.negm_ready = sem(n + "_negm_ready")
        self.mT_ready = sem(n + "_mT_ready")
        self.mT_out = sem(n + "_mT_out")
        self.m_in = sem(n + "_m_in")
        self.st_mm = sem(n + "_st_mm")
        self.exp_done = sem(n + "_exp_done")
        self.pv_done = sem(n + "_pv_done")
        self.o_out = sem(n + "_o_out")
        self.oT_ready = sem(n + "_oT_ready")
        if self.cross:
            self.den_ready = sem("cross_den_ready")
        self.rec_ready = sem(n + "_rec_ready")
        self.ao_ready = sem(n + "_ao_ready")
        self.aT_ready = sem(n + "_aT_ready")
        self.ahi_ready = sem(n + "_ahi_ready")
        self.alo_ready = sem(n + "_alo_ready")
        self.op_mm = sem(n + "_op_mm")
        self.y_ready = sem(n + "_y_ready")


def attention(nc, program, ins, sh, x2_dram):
    x_groups = ins.x.rearrange("(n b) s d -> n s b d", b=G)
    ctx_groups = ins.ctx.rearrange("(n b) s d -> n s b d", b=G)
    x2_groups = x2_dram.rearrange("(n b) s d -> n s b d", b=G)
    with ExitStack() as stack:
        sb, ps, sem = allocators(nc, stack, program)
        slf = Chain("self", sb, ps, sem, 0)
        crs = Chain("cross", sb, ps, sem, 4)
        cin = sb("ctx_in", [P, G, D])
        chl = sb("ctx_hl", [P, 2, KT, T], F16)
        earg = sb("earg", [P, G * H])
        ew = sb("ew", [P, G, H])
        ecnt = sb("ecnt", [P, G, H])
        ue = sb("ue", [P, G, D])
        nsum = sb("nsum", [P, QUADS, G, 4 * HD])
        dsum = sb("dsum", [P, QUADS, G * 4])
        yout = sb("yout", [P, G, D])
        primed = sem("primed")
        c_loaded, cT_ready, chi_ready, clo_ready = sem("c_loaded"), sem("cT_ready"), sem("chi_ready"), sem("clo_ready")
        earg_ready, ew_ready, ecnt_ready = sem("earg_ready"), sem("ew_ready"), sem("ecnt_ready")
        u_mm, ue_ready, stored = sem("u_mm"), sem("ue_ready"), sem("stored")
        ring = (0, 1, 3)
        turned = (0, 1, 3, 2)

        def src_ready(engine, ch, g):
            if ch.cross:
                engine.wait_ge(slf.y_ready, 2 * g + 2)
            else:
                engine.wait_ge(ch.loaded, 16 * g + 16)

        def stack_rows(engine, ch, g):
            engine.wait_ge(ch.qk_lo, 4 * g + 4)
            for j in range(FT):
                rows, to, p = slice(HD * j, HD * j + HD), HALF * (j % 2), j // 2
                block = [slice(to + HD * k, to + HD * k + HD) for k in range(3)]
                engine.dma_start(ch.stk[block[0], 0, p::4, :], ch.qk[rows, 2]).then_inc(ch.stacked, 16)
                engine.dma_start(ch.stk[block[0], 1, p::4, :], ch.qk[rows, 1]).then_inc(ch.stacked, 16)
                engine.dma_start(ch.stk[block[1], 0:2, p::4, :], ch.qk[rows, 0:2]).then_inc(ch.stacked, 16)
                engine.dma_start(ch.stk[block[2], 0:2, p::4, :], ch.qk[rows, 2:4]).then_inc(ch.stacked, 16)

        def stack_maxima(engine, ch, g):
            engine.wait_ge(ch.mT_out, g + 1)
            for r in range(2):
                engine.dma_start(ch.stk[HALF * r + STACK:HALF * (r + 1), 0, :, :],
                                 ch.negmT[:, :].unsqueeze(1).broadcast_to([H, PAIRS, T])).then_inc(ch.m_in, 16)

        def sp_step(sp, cg, sg):
            if sg is not None:
                x_group = x_groups[sg]
                wait(sp, slf.xn_ready, sg)
                wait(sp, slf.xb_ready, sg)
                sp.dma_start(slf.src[:, :, :], x_group).then_inc(slf.loaded, 16)
            if cg is not None:
                ctx_group = ctx_groups[cg]
                wait(sp, cT_ready, cg)
                sp.dma_start(cin[:, :, :], ctx_group).then_inc(c_loaded, 16)
                if not isinstance(cg, int) or cg:
                    sp_store(sp, cg - 1)
                stack_rows(sp, crs, cg)
            if sg is not None:
                stack_rows(sp, slf, sg)
            if cg is not None:
                stack_maxima(sp, crs, cg)
            if sg is not None:
                stack_maxima(sp, slf, sg)

        def sp_store(sp, cg):
            x2_group = x2_groups[cg]
            sp.wait_ge(crs.y_ready, 2 * cg + 2)
            sp.dma_start(x2_group, yout[:, :, :]).then_inc(stored, 16)

        def pool_step(pool, pairs):
            for ch, g in pairs:
                pool.wait_ge(ch.var_ready, g + 1)
                wait(pool, ch.xn_ready, g)
                nc.gpsimd.tensor_tensor(ch.rstd[:, :], ch.ve[:, :], sh.mhalf[:, :], ALU.pow).then_inc(ch.rstd_ready, 1)
            for ch, g in pairs:
                src_ready(pool, ch, g)
                wait(pool, ch.y_ready, 2 * g)
                nc.gpsimd.tensor_tensor(ch.xb[:, :, :], ch.src[:, :, :],
                                        sh.boB[:, ch.which:ch.which + 1, :].broadcast_to([P, G, D]),
                                        ALU.add).then_inc(ch.xb_ready, 1)

        def act_step(pairs):
            act = nc.scalar
            for ch, g in pairs:
                act.wait_ge(ch.xT_ready, g + 1)
                act.activation(ch.xhl[:, HI], ch.bk[:, 0:2, :], ACT.Copy).then_inc(ch.xhi_ready, 1)
                if ch.cross:
                    act.wait_ge(cT_ready, g + 1)
                    act.activation(chl[:, HI], ch.bk[:, 2:4, :], ACT.Copy).then_inc(chi_ready, 1)
            for n in range(4):
                for ch, g in pairs:
                    act.wait_ge(ch.qk_mm, 4 * g + n + 1)
                    if n == 0:
                        wait(act, ch.oT_ready, 4 * g)
                        wait(act, ch.stacked, 16 * STACK_DMAS * g)
                    act.activation(ch.qk[:, 2 - n // 2, n % 2], ch.bk[:, (2 + n) % 4, :], ACT.Identity,
                                   bias=sh.bcol[:, 2 * ch.which + n // 2, n % 2:n % 2 + 1]).then_inc(ch.qk_hi, 1)
            for ch, g in pairs:
                act.wait_ge(ch.mT_ready, g + 1)
                wait(act, ch.m_in, 32 * g)
                act.activation(ch.negmT[:, :], ch.bk[0:H, 0, 0:T // 2].bitcast(F16), ACT.Copy).then_inc(ch.mT_out, 1)
                if ch.cross:
                    act.wait_ge(earg_ready, g + 1)
                    act.activation(ew[:, :, :].rearrange("p b h -> p (b h)"), earg[:, :], ACT.Exp, scale=HD ** -0.5).then_inc(ew_ready, 1)
            for qd in range(QUADS + 1):
                for ch, g in pairs:
                    if qd < QUADS:
                        wait(act, ch.pv_done, 4 * g + qd - 1)
                        for jq in range(4):
                            n = 4 * qd + jq
                            act.wait_ge(ch.st_mm, 16 * g + n + 1)
                            act.activation(ch.prob[:, qd % 2, jq], ch.bk[:, ring[n % 3], :], ACT.Exp,
                                           scale=EXP_SCALE).then_inc(ch.exp_done, 1)
                    if qd:
                        act.wait_ge(ch.pv_done, 4 * g + qd)
                        if qd == 1:
                            act.wait_ge(ch.stacked, 16 * STACK_DMAS * (g + 1))
                        act.activation(ch.oT[:, qd - 1], ch.bk[:, 2, :], ACT.Copy).then_inc(ch.o_out, 1)
            for ch, g in pairs:
                act.wait_ge(ch.aT_ready, g + 1)
                act.activation(ch.xhl[:, HI], ch.bk[:, 0:2, :], ACT.Copy).then_inc(ch.ahi_ready, 1)

        def dve_step(pairs):
            dve = nc.vector
            for n, (ch, g) in enumerate(pairs):
                src_ready(dve, ch, g)
                for b in range(G):
                    if n and b == G - 1:
                        dve.wait_ge(pairs[0][0].stats_done, 4 * pairs[0][1] + 4)
                    dve.bn_stats(ch.stats[:, b], ch.src[:, b]).then_inc(ch.stats_done, 1)
            for n, (ch, g) in enumerate(pairs):
                if n == len(pairs) - 1 and not n:
                    dve.wait_ge(ch.stats_done, 4 * g + 4)
                for b in range(G):
                    last = dve.bn_aggr(ch.mv[:, b], ch.stats[:, b])
                last.then_inc(ch.moments, 1)
                if n < len(pairs) - 1:
                    dve.wait_ge(pairs[n + 1][0].stats_done, 4 * pairs[n + 1][1] + 4)
                dve.wait_ge(ch.moments, g + 1)
                dve.tensor_scalar(ch.ve[:, :], ch.mv[:, :, 1], LN_EPS, None, ALU.add).then_inc(ch.var_ready, 1)
            for ch, g in pairs:
                dve.wait_ge(ch.rstd_ready, g + 1)
                for b in range(G):
                    last = dve.tensor_scalar(ch.xn[:, b], ch.src[:, b], ch.mv[:, b, 0:1], ch.rstd[:, b:b + 1],
                                             ALU.subtract, ALU.mult)
                last.then_inc(ch.xn_ready, 1)
            for ch, g in pairs:
                dve.wait_ge(ch.xhi_ready, g + 1)
                dve.tensor_tensor(ch.xhl[:, LO], ch.bk[:, 0:2, :], ch.xhl[:, HI], ALU.subtract).then_inc(ch.xlo_ready, 1)
                if ch.cross:
                    dve.wait_ge(chi_ready, g + 1)
                    dve.tensor_tensor(chl[:, LO], ch.bk[:, 2:4, :], chl[:, HI], ALU.subtract).then_inc(clo_ready, 1)
            for n in range(4):
                for ch, g in pairs:
                    dve.wait_ge(ch.qk_hi, 4 * g + n + 1)
                    dve.scalar_tensor_tensor(ch.qk[:, 3 * (n // 2), n % 2], ch.bk[:, (2 + n) % 4, :],
                                             sh.bcol[:, 2 * ch.which + n // 2, n % 2:n % 2 + 1],
                                             ch.qk[:, 2 - n // 2, n % 2], ALU.add, ALU.subtract).then_inc(ch.qk_lo, 1)
            for n in range(2):
                for ch, g in pairs:
                    dve.wait_ge(ch.v_mm, 2 * g + n + 1)
                    dve.tensor_tensor(ch.vals[:, 2 * n:2 * n + 2, :, 0:HD].rearrange("p b h d -> p (b h) d"),
                                      ch.bk[:, 2 + n, :].rearrange("p (a d) -> p a d", d=HD),
                                      sh.bv2[:, ch.which].rearrange("p b (h d) -> p (b h) d", d=HD), ALU.add).then_inc(ch.v_ready, 1)
            for n in range(16):
                for ch, g in pairs:
                    dve.wait_ge(ch.s_mm, 16 * g + n + 1)
                    first = 8 * (n // 2) + n % 2
                    dve.tensor_reduce(ch.mx[:, first:first + 7:2], ch.bk[:, n % 4, :].rearrange("p (h k) -> p h k", h=4),
                                      AX.X, ALU.max).then_inc(ch.max_done, 1)
            for ch, g in pairs:
                dve.wait_ge(ch.max_done, 16 * g + 16)
                if ch.cross:
                    dve.tensor_scalar(ch.negm[:, :], ch.mx[:, :], sh.mfloor[:, :], -1.0 / SHIFT, ALU.max, ALU.mult).then_inc(ch.negm_ready, 1)
                    dve.wait_ge(ch.negm_ready, g + 1)
                    dve.tensor_scalar(earg[:, :], ch.negm[:, :], 0.0, MASKED * HD ** 0.5, ALU.min, ALU.add).then_inc(earg_ready, 1)
                else:
                    dve.tensor_scalar(ch.negm[:, :], ch.mx[:, :], -1.0 / SHIFT, None, ALU.mult).then_inc(ch.negm_ready, 1)
            for ch, g in pairs:
                if ch.cross:
                    dve.wait_ge(ew_ready, g + 1)
                    dve.tensor_scalar(ecnt[:, :, :], ew[:, :, :], sh.cntW[:, :], None, ALU.mult).then_inc(ecnt_ready, 1)
                    for n in range(2):
                        dve.wait_ge(u_mm, 2 * g + n + 1)
                        dve.tensor_tensor(ue[:, 2 * n:2 * n + 2].rearrange("p b (h d) -> p (b h) d", d=HD),
                                          ch.bk[:, (1, 3)[n], :].rearrange("p (a d) -> p a d", d=HD),
                                          ew[:, 2 * n:2 * n + 2].rearrange("p b h -> p (b h)").unsqueeze(2).broadcast_to([P, 2 * H, HD]),
                                          ALU.mult).then_inc(ue_ready, 1)
            for qd in range(QUADS):
                for ch, g in pairs:
                    dve.wait_ge(ch.oT_ready, 4 * g + qd + 1)
                    o = ch.bk[:, turned[qd], :].rearrange("p (b h c) -> p b h c", b=G, h=4)
                    den = ch.bk[:, turned[qd], HD::VW]
                    if ch.cross:
                        dve.wait_ge(ue_ready, 2 * g + 2)
                        dve.wait_ge(ecnt_ready, g + 1)
                        dve.tensor_tensor(nsum[:, qd].rearrange("p b (h d) -> p b h d", d=HD), o[:, :, :, 0:HD],
                                          ue[:, :, qd * 4 * HD:(qd + 1) * 4 * HD].rearrange("p b (h d) -> p b h d", d=HD), ALU.add)
                        dve.tensor_tensor(dsum[:, qd].rearrange("p (b h) -> p b h", b=G), o[:, :, :, HD],
                                          ecnt[:, :, 4 * qd:4 * qd + 4], ALU.add).then_inc(ch.den_ready, 1)
                        dve.wait_ge(ch.den_ready, 4 * g + qd + 1)
                        den = dsum[:, qd]
                    dve.reciprocal(ch.rec[:, qd], den).then_inc(ch.rec_ready, 1)
                    dve.wait_ge(ch.rec_ready, 4 * g + qd + 1)
                    num = nsum[:, qd].rearrange("p b (h d) -> p b h d", d=HD) if ch.cross else o[:, :, :, 0:HD]
                    dve.tensor_tensor(ch.xn[:, :, qd * 4 * HD:(qd + 1) * 4 * HD].rearrange("p b (h d) -> p b h d", d=HD), num,
                                      ch.rec[:, qd].rearrange("p (b h) -> p b h", b=G).unsqueeze(3).broadcast_to([P, G, 4, HD]),
                                      ALU.mult).then_inc(ch.ao_ready, 1)
            for ch, g in pairs:
                dve.wait_ge(ch.ahi_ready, g + 1)
                dve.tensor_tensor(ch.xhl[:, LO], ch.bk[:, 0:2, :], ch.xhl[:, HI], ALU.subtract).then_inc(ch.alo_ready, 1)
            for n in range(2):
                for ch, g in pairs:
                    dve.wait_ge(ch.op_mm, 2 * g + n + 1)
                    if n == 0:
                        dve.wait_ge(ch.xb_ready, g + 1)
                        if ch.cross:
                            wait(dve, stored, 16 * g)
                        else:
                            wait(dve, crs.xb_ready, g)
                            wait(dve, crs.xn_ready, g)
                    y = yout if ch.cross else crs.src
                    dve.scalar_tensor_tensor(y[:, 2 * n:2 * n + 2].rearrange("p b d -> p (b d)"), ch.bk[:, 2 + n, :], 1.0 / WS,
                                             ch.xb[:, 2 * n:2 * n + 2].rearrange("p b d -> p (b d)"),
                                             ALU.mult, ALU.add).then_inc(ch.y_ready, 1)

        def tile_product(ch, bank, w, tile, moving):
            for n, (a, wp) in enumerate(SPLITS):
                for kt in range(KT):
                    last = nc.tensor.matmul(ch.bk[:, bank, :], sh.WT[:, w, wp, kt, tile * P:(tile + 1) * P], moving[:, a, kt, :],
                                            start=(n == 0 and kt == 0), stop=(n == 2 and kt == KT - 1))
            return last

        def token_product(ch, bank, w, b, tokens):
            for n, (a, wp) in enumerate(SPLITS):
                for kt in range(KT):
                    last = nc.tensor.matmul(ch.bk[:, bank, (b % 2) * D:(b % 2 + 1) * D], tokens[:, a, kt, b * S:(b + 1) * S],
                                            sh.WT[:, w, wp, kt, :], start=(n == 0 and kt == 0), stop=(n == 2 and kt == KT - 1))
            return last

        def turn(ch, bank, src):
            for kt in range(KT):
                for b in range(G):
                    last = nc.tensor.transpose(ch.bk[:, bank + kt, b * S:(b + 1) * S], src[:, b, kt * P:(kt + 1) * P], sh.ident[:, :])
            return last

        def pe_step(pairs):
            pe = nc.tensor
            for ch, g in pairs:
                pe.wait_ge(ch.xn_ready, g + 1)
                turn(ch, 0, ch.xn).then_inc(ch.xT_ready, 1)
                if ch.cross:
                    pe.wait_ge(c_loaded, 16 * g + 16)
                    wait(pe, ch.y_ready, 2 * g)
                    turn(ch, 2, cin).then_inc(cT_ready, 1)
            for n in range(6):
                for ch, g in pairs:
                    other = chl if ch.cross else ch.xhl
                    if n == 0:
                        pe.wait_ge(ch.xlo_ready, g + 1)
                        if ch.cross:
                            pe.wait_ge(clo_ready, g + 1)
                        else:
                            wait(pe, ch.y_ready, 2 * g)
                    if n < 4:
                        tile_product(ch, (2 + n) % 4, (ch.wq, ch.wk)[n // 2], n % 2, other if n > 1 else ch.xhl).then_inc(ch.qk_mm, 1)
                    else:
                        pe.wait_ge(ch.qk_lo, 4 * g + n - 3)
                        for b in (2 * n - 8, 2 * n - 7):
                            last = token_product(ch, n - 2, ch.wv, b, other)
                        last.then_inc(ch.v_mm, 1)
            for m in range(8):
                b, eight = divmod(m, 2)
                for ch, g in pairs:
                    if m == 0:
                        pe.wait_ge(ch.stacked, 16 * STACK_DMAS * (g + 1))
                    for r in range(2):
                        n = 2 * m + r
                        if n in (2, 3):
                            pe.wait_ge(ch.v_ready, 2 * g + n - 1)
                        if n > 3:
                            pe.wait_ge(ch.max_done, 16 * g + n - 3)
                        if ch.cross:
                            pe.matmul(ch.bk[:, n % 4, :], sh.identb[:, :], sh.maskB4[:, :, :], start=True, stop=False, skip_group_check=True)
                    for j in range(4):
                        for r in range(2):
                            rows = slice(HALF * r, HALF * r + STACK)
                            last = pe.matmul(ch.bk[:, (2 * m + r) % 4, j * S:(j + 1) * S], ch.stk[rows, 0, 4 * eight + j, b * S:(b + 1) * S],
                                             ch.stk[rows, 1, 4 * eight + j, b * S:(b + 1) * S], start=not ch.cross, stop=True, skip_group_check=True)
                            if j == 3:
                                last.then_inc(ch.s_mm, 1)
            for ch, g in pairs:
                pe.wait_ge(ch.negm_ready, g + 1)
                for b in range(G):
                    last = pe.transpose(ch.bk[0:H, 0, b * S // 2:(b + 1) * S // 2].bitcast(F16), ch.negm[:, b * H:(b + 1) * H], sh.ident16[:, :])
                last.then_inc(ch.mT_ready, 1)
                if ch.cross:
                    for b in range(G):
                        last = pe.matmul(ch.bk[:, (1, 3)[b // 2], (b % 2) * D:(b % 2 + 1) * D], sh.maskcT[:, :],
                                         ch.vals[:, b, :, 0:HD], start=True, stop=True)
                        if b % 2:
                            last.then_inc(u_mm, 1)
            for qd in range(QUADS + 1):
                for ch, g in pairs:
                    if qd < QUADS:
                        for pair in (2 * qd, 2 * qd + 1):
                            for r in range(2):
                                n = 2 * pair + r
                                if n == 0:
                                    pe.wait_ge(ch.m_in, 32 * (g + 1))
                                    pe.wait_ge(ch.mT_out, g + 1)
                                if n in (1, 2) and ch.cross:
                                    pe.wait_ge(ue_ready, 2 * g + n)
                                if n > 2:
                                    pe.wait_ge(ch.exp_done, 16 * g + n - 2)
                                if ch.cross:
                                    pe.matmul(ch.bk[:, ring[n % 3], :], sh.identb[:, :], sh.maskBT4[:, :, :], start=True, stop=False, skip_group_check=True)
                            for b in range(G):
                                for r in range(2):
                                    rows = slice(HALF * r, HALF * (r + 1))
                                    last = pe.matmul(ch.bk[:, ring[(2 * pair + r) % 3], b * S:(b + 1) * S], ch.stk[rows, 1, pair, b * S:(b + 1) * S],
                                                     ch.stk[rows, 0, pair, b * S:(b + 1) * S], start=not ch.cross, stop=True, skip_group_check=True)
                                    if b == G - 1:
                                        last.then_inc(ch.st_mm, 1)
                    if qd:
                        pe.wait_ge(ch.exp_done, 16 * g + 4 * qd)
                        if qd > 1:
                            pe.wait_ge(ch.o_out, 4 * g + qd - 1)
                        for b in range(G):
                            for jq in range(4):
                                last = pe.matmul(ch.bk[32 * jq:32 * jq + VW, 2, b * S:(b + 1) * S], ch.vals[:, b, 4 * qd - 4 + jq, :],
                                                 ch.prob[:, (qd - 1) % 2, jq, b * S:(b + 1) * S], start=True, stop=True, skip_group_check=True)
                        last.then_inc(ch.pv_done, 1)
            for qd in range(QUADS):
                for ch, g in pairs:
                    pe.wait_ge(ch.o_out, 4 * g + 4 if qd == 3 else 4 * g + qd + 1)
                    for b in range(G):
                        last = pe.transpose(ch.bk[:, turned[qd], b * S:(b + 1) * S], ch.oT[:, qd, b * S:(b + 1) * S], sh.ident[:, :])
                    last.then_inc(ch.oT_ready, 1)
            for ch, g in pairs:
                pe.wait_ge(ch.ao_ready, 4 * g + 4)
                turn(ch, 0, ch.xn).then_inc(ch.aT_ready, 1)
            for n in range(2):
                for ch, g in pairs:
                    pe.wait_ge(ch.alo_ready, g + 1)
                    for b in (2 * n, 2 * n + 1):
                        last = token_product(ch, 2 + n, ch.wo, b, ch.xhl)
                    last.then_inc(ch.op_mm, 1)

        def both(i):
            return [(crs, i), (slf, i + 1)]

        with nc.Block() as block:
            @block.sync
            def _(sp):
                sp.wait_ge(primed, 8)
                sp_step(sp, None, 0)
                sp_step(sp, 0, 1)
                with sp.Fori(1, NG - 1) as i:
                    sp_step(sp, i, i + 1)
                sp_step(sp, NG - 1, None)
                sp_store(sp, NG - 1)
                sp.wait_ge(stored, 16 * NG)

            @block.gpsimd
            def _(pool):
                for ch in (slf, crs):
                    nc.gpsimd.memset(ch.vals[:, :, :, :], 0.0).then_inc(primed, 1)
                    nc.gpsimd.memset(ch.stk[:, 1, :, :], 0.0).then_inc(primed, 1)
                for r in range(2):
                    pool.wait_ge(primed, 4 + 2 * r)
                    for ch in (slf, crs):
                        nc.gpsimd.affine_select(out=ch.stk[:, 1, :, :], in_=ch.stk[:, 1, :, :], compare_op=ALU.not_equal, fill=SHIFT,
                                                base=-(HALF * r + STACK + r), pattern=[[-2, PAIRS], [0, T]],
                                                channel_multiplier=1).then_inc(primed, 1)
                for ch in (slf, crs):
                    nc.gpsimd.memset(ch.vals[:, :, :, HD:HD + 1], WS).then_inc(primed, 1)
                pool_step(pool, [(slf, 0)])
                pool_step(pool, both(0))
                with pool.Fori(1, NG - 1) as i:
                    pool_step(pool, both(i))
                pool_step(pool, [(crs, NG - 1)])

            @block.scalar
            def _(act):
                act_step([(slf, 0)])
                act_step(both(0))
                with act.Fori(1, NG - 1) as i:
                    act_step(both(i))
                act_step([(crs, NG - 1)])

            @block.vector
            def _(dve):
                dve.wait_ge(primed, 10)
                dve_step([(slf, 0)])
                dve_step(both(0))
                with dve.Fori(1, NG - 1) as i:
                    dve_step(both(i))
                dve_step([(crs, NG - 1)])

            @block.tensor
            def _(pe):
                pe.wait_ge(primed, 10)
                pe_step([(slf, 0)])
                pe_step(both(0))
                with pe.Fori(1, NG - 1) as i:
                    pe_step(both(i))
                pe_step([(crs, NG - 1)])


class Lane:

    def __init__(self, n, sb, ps, sem):
        self.src = sb(n + "_src", [P, G, D])
        self.stats = sb(n + "_stats", [P, G, 6])
        self.mv = sb(n + "_mv", [P, G, 2])
        self.ve = sb(n + "_ve", [P, G])
        self.rstd = sb(n + "_rstd", [P, G])
        self.xn = sb(n + "_xn", [P, G, D])
        self.xc = sb(n + "_xc", [P, G, D])
        self.xhl = sb(n + "_xhl", [P, 2, KT, T], F16)
        self.hid = sb(n + "_hid", [P, 2, F])
        self.hstats = sb(n + "_hstats", [P, G, 2, 6])
        self.hmv = sb(n + "_hmv", [P, G, 2])
        self.hve = sb(n + "_hve", [P, G])
        self.hrstd = sb(n + "_hrstd", [P, G])
        self.cen = sb(n + "_cen", [P, 2, F])
        self.chl = sb(n + "_chl", [P, 2, 2, FT, S], F16)
        self.y = sb(n + "_y", [P, G, D])
        self.bk = ps(n + "_bk", [P, 4, 512])
        self.loaded = sem(n + "_loaded")
        self.stats_done = sem(n + "_stats_done")
        self.moments = sem(n + "_moments")
        self.var_ready = sem(n + "_var_ready")
        self.rstd_ready = sem(n + "_rstd_ready")
        self.xn_ready = sem(n + "_xn_ready")
        self.xc_ready = sem(n + "_xc_ready")
        self.xT_ready = sem(n + "_xT_ready")
        self.xhi_ready = sem(n + "_xhi_ready")
        self.xlo_ready = sem(n + "_xlo_ready")
        self.h_mm = sem(n + "_h_mm")
        self.hid_ready = sem(n + "_hid_ready")
        self.hstats_done = sem(n + "_hstats_done")
        self.hmv_ready = sem(n + "_hmv_ready")
        self.cen_ready = sem(n + "_cen_ready")
        self.hve_ready = sem(n + "_hve_ready")
        self.hrstd_ready = sem(n + "_hrstd_ready")
        self.cT_ready = sem(n + "_cT_ready")
        self.chi_ready = sem(n + "_chi_ready")
        self.clo_ready = sem(n + "_clo_ready")
        self.y_mm = sem(n + "_y_mm")
        self.y_ready = sem(n + "_y_ready")
        self.stored = sem(n + "_stored")


def ffn(nc, program, sh, x2_dram, out):
    x2_groups = x2_dram.rearrange("(n b) s d -> n s b d", b=G)
    out_groups = out.rearrange("(n b) s d -> n s b d", b=G)
    with ExitStack() as stack:
        sb, ps, sem = allocators(nc, stack, program)
        lanes = [Lane("even", sb, ps, sem), Lane("odd", sb, ps, sem)]
        STEPS = NG // 2
        held = sb("held", [P, 1])

        def sp_load(sp, i):
            for c, ln in enumerate(lanes):
                x2_group = x2_groups[2 * i + c]
                wait(sp, ln.xn_ready, i)
                wait(sp, ln.xc_ready, i)
                sp.dma_start(ln.src[:, :, :], x2_group).then_inc(ln.loaded, 16)

        def sp_store(sp, i):
            for c, ln in enumerate(lanes):
                out_group = out_groups[2 * i + c]
                sp.wait_ge(ln.y_ready, 4 * i + 4)
                sp.dma_start(out_group, ln.y[:, :, :]).then_inc(ln.stored, 16)

        def pool_step(pool, i):
            for ln in lanes:
                pool.wait_ge(ln.var_ready, i + 1)
                wait(pool, ln.xn_ready, i)
                nc.gpsimd.tensor_tensor(ln.rstd[:, :], ln.ve[:, :], sh.mhalf[:, :], ALU.pow).then_inc(ln.rstd_ready, 1)
            for ln in lanes:
                pool.wait_ge(ln.loaded, 16 * i + 16)
                wait(pool, ln.y_ready, 4 * i)
                nc.gpsimd.tensor_tensor(ln.xc[:, :, :], ln.src[:, :, :], sh.c2B[:, :].unsqueeze(1).broadcast_to([P, G, D]),
                                        ALU.add).then_inc(ln.xc_ready, 1)
            for b in range(G):
                for ln in lanes:
                    pool.wait_ge(ln.hve_ready, 4 * i + b + 1)
                    nc.gpsimd.tensor_tensor(ln.hrstd[:, b:b + 1], ln.hve[:, b:b + 1], sh.mhalf[:, 0:1], ALU.pow).then_inc(ln.hrstd_ready, 1)

        def act_step(i):
            act = nc.scalar
            for ln in lanes:
                act.wait_ge(ln.xT_ready, i + 1)
                act.activation(ln.xhl[:, HI], ln.bk[:, 0:2, :], ACT.Copy).then_inc(ln.xhi_ready, 1)
            for b in range(G + 1):
                for ln in lanes:
                    if b < G:
                        o = 2 * (b % 2)
                        act.wait_ge(ln.h_mm, 4 * i + b + 1)
                        wait(act, ln.cT_ready, 4 * i + b - 1)
                        act.activation(ln.hid[:, b % 2].rearrange("p (a h) -> p a h", a=2), ln.bk[:, o:o + 2, :], ACT.Gelu).then_inc(ln.hid_ready, 1)
                    if b:
                        c = b - 1
                        o = 2 * (c % 2)
                        act.wait_ge(ln.cT_ready, 4 * i + c + 1)
                        wait(act, ln.y_mm, 4 * i + c - 1)
                        act.activation(ln.chl[:, c % 2, HI].rearrange("p (a t) s -> p a (t s)", a=2), ln.bk[:, o:o + 2, :], ACT.Copy).then_inc(ln.chi_ready, 1)

        def dve_step(i):
            dve = nc.vector
            for n, ln in enumerate(lanes):
                dve.wait_ge(ln.loaded, 16 * i + 16)
                for b in range(G):
                    if n and b == G - 1:
                        dve.wait_ge(lanes[0].stats_done, 4 * i + 4)
                    dve.bn_stats(ln.stats[:, b], ln.src[:, b]).then_inc(ln.stats_done, 1)
            for n, ln in enumerate(lanes):
                for b in range(G):
                    last = dve.bn_aggr(ln.mv[:, b], ln.stats[:, b])
                last.then_inc(ln.moments, 1)
                if n == 0:
                    dve.wait_ge(lanes[1].stats_done, 4 * i + 4)
                dve.wait_ge(ln.moments, i + 1)
                dve.tensor_scalar(ln.ve[:, :], ln.mv[:, :, 1], LN_EPS, None, ALU.add).then_inc(ln.var_ready, 1)
            for ln in lanes:
                dve.wait_ge(ln.rstd_ready, i + 1)
                for b in range(G):
                    last = dve.tensor_scalar(ln.xn[:, b], ln.src[:, b], ln.mv[:, b, 0:1], ln.rstd[:, b:b + 1],
                                             ALU.subtract, ALU.mult)
                last.then_inc(ln.xn_ready, 1)
            for ln in lanes:
                dve.wait_ge(ln.xhi_ready, i + 1)
                dve.tensor_tensor(ln.xhl[:, LO], ln.bk[:, 0:2, :], ln.xhl[:, HI], ALU.subtract).then_inc(ln.xlo_ready, 1)
            for b in range(G + 2):
                for ln in lanes:
                    if b > 1:
                        c = b - 2
                        dve.wait_ge(ln.y_mm, 4 * i + c + 1)
                        dve.wait_ge(ln.hrstd_ready, 4 * i + c + 1)
                        if c == 0:
                            dve.wait_ge(ln.xc_ready, i + 1)
                            wait(dve, ln.stored, 16 * i)
                        dve.scalar_tensor_tensor(ln.y[:, c], ln.bk[:, 2 * (c % 2), 0:D], ln.hrstd[:, c:c + 1], ln.xc[:, c],
                                                 ALU.mult, ALU.add).then_inc(ln.y_ready, 1)
                    if b < G:
                        m = 4 * i + b + 1
                        dve.wait_ge(ln.hid_ready, m)
                        for a in range(2):
                            last = dve.bn_stats(ln.hstats[:, b, a], ln.hid[:, b % 2, a * (F // 2):(a + 1) * (F // 2)])
                        last.then_inc(ln.hstats_done, 1)
                        dve.wait_ge(ln.hstats_done, m)
                        dve.memset(held[:, :], 0.0)
                        dve.bn_aggr(ln.hmv[:, b], ln.hstats[:, b].rearrange("p a s -> p (a s)")).then_inc(ln.hmv_ready, 1)
                        dve.wait_ge(ln.hmv_ready, m)
                        dve.scalar_tensor_tensor(ln.cen[:, b % 2], ln.hid[:, b % 2], ln.hmv[:, b, 0:1], sh.lnwB[:, :],
                                                 ALU.subtract, ALU.mult).then_inc(ln.cen_ready, 1)
                        dve.tensor_scalar(ln.hve[:, b:b + 1], ln.hmv[:, b, 1:2], LN_EPS, None, ALU.add).then_inc(ln.hve_ready, 1)
                    if 0 < b <= G:
                        c = b - 1
                        dve.wait_ge(ln.chi_ready, 4 * i + c + 1)
                        dve.tensor_tensor(ln.chl[:, c % 2, LO].rearrange("p (a t) s -> p a (t s)", a=2), ln.bk[:, 2 * (c % 2):2 * (c % 2) + 2, :],
                                          ln.chl[:, c % 2, HI].rearrange("p (a t) s -> p a (t s)", a=2), ALU.subtract).then_inc(ln.clo_ready, 1)

        def pe_step(i):
            pe = nc.tensor
            for ln in lanes:
                pe.wait_ge(ln.xn_ready, i + 1)
                wait(pe, ln.y_ready, 4 * i)
                for kt in range(KT):
                    for b in range(G):
                        last = pe.transpose(ln.bk[:, kt, b * S:(b + 1) * S], ln.xn[:, b, kt * P:(kt + 1) * P], sh.ident[:, :])
                last.then_inc(ln.xT_ready, 1)
            for b in range(G + 2):
                for ln in lanes:
                    if b > 1:
                        c = b - 2
                        pe.wait_ge(ln.clo_ready, 4 * i + c + 1)
                        for part in (HI, LO):
                            for t in range(FT):
                                last = pe.matmul(ln.bk[:, 2 * (c % 2), 0:D], ln.chl[:, c % 2, part, t], sh.wpT[:, t],
                                                 start=(part == HI and t == 0), stop=(part == LO and t == FT - 1))
                        last.then_inc(ln.y_mm, 1)
                    if b < G:
                        if b == 0:
                            pe.wait_ge(ln.xlo_ready, i + 1)
                        if b > 1:
                            pe.wait_ge(ln.y_ready, 4 * i + b - 1)
                        for a in range(2):
                            for part in (HI, LO):
                                for kt in range(KT):
                                    last = pe.matmul(ln.bk[:, 2 * (b % 2) + a, :], ln.xhl[:, part, kt, b * S:(b + 1) * S],
                                                     sh.wfcT[:, kt, a * 512:(a + 1) * 512],
                                                     start=(part == HI and kt == 0), stop=(part == LO and kt == KT - 1))
                        last.then_inc(ln.h_mm, 1)
                    if 0 < b <= G:
                        c = b - 1
                        pe.wait_ge(ln.cen_ready, 4 * i + c + 1)
                        for t in range(FT):
                            last = pe.transpose(ln.bk[:, 2 * (c % 2) + t // 4, (t % 4) * S:(t % 4 + 1) * S],
                                                ln.cen[:, c % 2, t * P:(t + 1) * P], sh.ident[:, :])
                        last.then_inc(ln.cT_ready, 1)

        with nc.Block() as block:
            @block.sync
            def _(sp):
                sp_load(sp, 0)
                sp_load(sp, 1)
                sp_store(sp, 0)
                with sp.Fori(1, STEPS - 1) as i:
                    sp_load(sp, i + 1)
                    sp_store(sp, i)
                sp_store(sp, STEPS - 1)
                for ln in lanes:
                    sp.wait_ge(ln.stored, 16 * STEPS)

            @block.gpsimd
            def _(pool):
                pool_step(pool, 0)
                with pool.Fori(1, STEPS) as i:
                    pool_step(pool, i)

            @block.scalar
            def _(act):
                act_step(0)
                with act.Fori(1, STEPS) as i:
                    act_step(i)

            @block.vector
            def _(dve):
                dve_step(0)
                with dve.Fori(1, STEPS) as i:
                    dve_step(i)

            @block.tensor
            def _(pe):
                pe_step(0)
                with pe.Fori(1, STEPS) as i:
                    pe_step(i)


INPUTS = ("x", "ctx_1024", "mask_1x1xSxS2_ik1",
          "L0_attn_Wq", "L0_attn_bq", "L0_attn_Wk", "L0_attn_bk", "L0_attn_Wv", "L0_attn_bv", "L0_attn_Wo", "L0_attn_bo",
          "L0_xattn_wq_w", "L0_xattn_wq_b", "L0_xattn_wk_w", "L0_xattn_wk_b", "L0_xattn_wv_w", "L0_xattn_wv_b",
          "L0_xattn_wo_w", "L0_xattn_wo_b", "L0_ffn_W_fc", "L0_ffn_ln_w", "L0_ffn_ln_b", "L0_ffn_W_proj")


def kernel(**inputs):
    import numpy as np
    import concourse.bacc as bacc
    from concourse.bass_utils import run_bass_kernel_spmd

    nc = bacc.Bacc("TRN2", target_bir_lowering=False, num_devices=1)
    arrays, aps = {}, []
    for name in INPUTS:
        a = np.ascontiguousarray(inputs[name])
        arrays["in_" + name] = a
        aps.append(nc.dram_tensor("in_" + name, a.shape, mybir.dt.from_np(a.dtype), kind="ExternalInput").ap())
    out = nc.dram_tensor("out_0", (B, S, D), F32, kind="ExternalOutput").ap()
    decoder_layer_kernel(nc, Inputs(*aps), out)
    result = run_bass_kernel_spmd(nc, [arrays], core_ids=[0])
    return result.results[0]["out_0"]
```

```python
from contextlib import ExitStack

import concourse.bass as bass
from concourse import mybir

F32, F16, BF16, I32 = mybir.dt.float32, mybir.dt.float16, mybir.dt.bfloat16, mybir.dt.int32
ALU = mybir.AluOpType
ACT = mybir.ActivationFunctionType
AX = mybir.AxisListType

P = 128
B, S, D = 128, 128, 256
H = 16
HD = D // H
F = 1024
G = 4
NG = B // G
T = G * S
KT = D // P
FT = F // P
PAIRS = H // 2
HALF = 64
STACK = 3 * HD
QUADS = H // 4
VW = 32
WS = 8.0
SHIFT = WS * WS
EXP_SCALE = 1.0 / (HD ** 0.5 * SHIFT)
LN_EPS = 1e-5
GAMMA_EPS = 1e-6
MASKED = 1e-9
NEG = -1e30
HI, LO = 0, 1
SPLITS = ((HI, HI), (LO, HI), (HI, LO))

SQ, SK, SV, SO, XQ, XK, XV, XO = range(8)
STACK_DMAS = 3 * FT


class Inputs:

    def __init__(self, x, ctx, mask, sWq, sbq, sWk, sbk, sWv, sbv, sWo, sbo,
                 xWq, xbq, xWk, xbk, xWv, xbv, xWo, xbo, Wfc, lnw, lnb, Wp):
        self.x, self.ctx, self.mask = x, ctx, mask
        self.weights = [sWq, sWk, sWv, sWo, xWq, xWk, xWv, xWo]
        self.qk_biases = [sbq, sbk, xbq, xbk]
        self.v_biases, self.o_biases = [sbv, xbv], [sbo, xbo]
        self.Wfc, self.lnw, self.lnb, self.Wp = Wfc, lnw, lnb, Wp


class Shared:

    def __init__(self, sb):
        self.WT = sb("WT", [P, 8, 2, KT, D], F16)
        self.wfcT = sb("wfcT", [P, KT, F], F16)
        self.wpT = sb("wpT", [P, FT, D], F16)
        self.bcol = sb("bcol", [P, 4, KT])
        self.boB = sb("boB", [P, 2, D])
        self.lnwB = sb("lnwB", [P, F])
        self.c2B = sb("c2B", [P, D])
        self.ident = sb("ident", [P, P])
        self.ident16 = sb("ident16", [P, P], F16)
        self.identb = sb("identb", [P, P], BF16)
        self.mhalf = sb("mhalf", [P, G])
        self.maskB4 = sb("maskB4", [P, 4, S], BF16)
        self.maskBT4 = sb("maskBT4", [P, G, S], BF16)
        self.maskcT = sb("maskcT", [P, S])
        self.cntW = sb("cntW", [P, 1])
        self.mfloor = sb("mfloor", [P, 1])


def allocators(nc, stack, program):
    sb = lambda name, shape, dt=F32: stack.enter_context(nc.sbuf_tensor(name, shape, dt))
    ps = lambda name, shape, dt=F32: stack.enter_context(nc.psum_tensor(name, shape, dt))
    sem = lambda name: program.enter_context(nc.semaphore(name))
    return sb, ps, sem


def wait(engine, sem, count):
    if not isinstance(count, int) or count > 0:
        engine.wait_ge(sem, count)


def decoder_layer_kernel(nc, ins, out):
    x2_dram = nc.dram_tensor("x2_scratch", (B, S, D), F32, kind="Internal").ap()
    with ExitStack() as stack:
        sb, _, _ = allocators(nc, stack, stack)
        sh = Shared(sb)
        setup(nc, stack, ins, sh)
        attention(nc, stack, ins, sh, x2_dram)
        ffn(nc, stack, sh, x2_dram, out)


def setup(nc, program, ins, sh):
    WT, wfcT, wpT, bcol, boB, lnwB, c2B = sh.WT, sh.wfcT, sh.wpT, sh.bcol, sh.boB, sh.lnwB, sh.c2B
    ident, ident16, identb, mhalf = sh.ident, sh.ident16, sh.identb, sh.mhalf
    maskB4, maskBT4, maskcT, cntW, mfloor = sh.maskB4, sh.maskBT4, sh.maskcT, sh.cntW, sh.mfloor

    with ExitStack() as stack:
        sb, ps, sem = allocators(nc, stack, program)
        wnat = sb("wnat", [P, 8, KT, D])
        fnat = sb("fnat", [P, 2, F * KT])
        neg = sb("neg", [P, 2, F * KT])
        junk = sb("junk", [P, F * KT])
        wpT32 = sb("wpT32", [P, FT, D])
        lnb_col = sb("lnb_col", [P, FT])
        bv_col = sb("bv_col", [P, 2 * KT])
        bvB = sb("bvB", [P, 2, 2 * KT, P], F16)
        lnbB = sb("lnbB", [P, FT, P])
        ones = sb("ones", [P, P])
        asum = sb("asum", [P, 2])
        thr = sb("thr", [P, 2])
        nthr = sb("nthr", [P, 2])
        imask = sb("imask", [P, S], I32)
        maskc = sb("maskc", [P, S])
        bank = ps("setup_bank", [P, 8, 512])

        w_in = sem("w_in")
        f_in, small_in, mask_in = sem("f_in"), sem("small_in"), sem("mask_in")
        zeroed, consts = sem("zeroed"), sem("consts")
        w_T, w_hi, w_lo = sem("w_T"), sem("w_hi"), sem("w_lo")
        abs_done, total_done, gamma_done, thr_done = sem("abs_done"), sem("total_done"), sem("gamma_done"), sem("thr_done")
        neg_done, tern_done, f_T, f_out = sem("neg_done"), sem("tern_done"), sem("f_T"), sem("f_out")
        lnb_done, c2_mm, c2_done = sem("lnb_done"), sem("c2_mm"), sem("c2_done")
        m_done, mc_done, m_T, m_out, cnt_done = sem("m_done"), sem("mc_done"), sem("m_T"), sem("m_out"), sem("cnt_done")
        scaled, bv_split, bo_mm, bo_done = sem("scaled"), sem("bv_split"), sem("bo_mm"), sem("bo_done")
        NSMALL = 4 + 2 + 2 + 1 + 1

        with nc.Block() as block:
            @block.sync
            def _(sp):
                for n, w in enumerate(ins.weights):
                    sp.dma_start(wnat[:, n], w.rearrange("(m p) i -> p m i", p=P)).then_inc(w_in, 16)
                for n, b in enumerate(ins.qk_biases):
                    sp.dma_start(bcol[:, n], b.rearrange("(m p) -> p m", p=P), allow_slow_non_contiguous=True).then_inc(small_in, 16)
                for n, b in enumerate(ins.v_biases):
                    sp.dma_start(bv_col[:, n * KT:(n + 1) * KT], b.rearrange("(m p) -> p m", p=P), allow_slow_non_contiguous=True).then_inc(small_in, 16)
                sp.dma_start(lnb_col[:, :], ins.lnb.rearrange("(t p) -> p t", p=P), allow_slow_non_contiguous=True).then_inc(small_in, 16)

            @block.scalar
            def _(act):
                act.dma_start(fnat[:, 0], ins.Wfc.rearrange("(t p) d -> p t d", p=P)).then_inc(f_in, 16)
                act.dma_start(fnat[:, 1], ins.Wp.rearrange("(t p) h -> p t h", p=P)).then_inc(f_in, 16)
                act.dma_start(imask[:, :], ins.mask[0, 0]).then_inc(mask_in, 16)
                for n in range(2):
                    act.dma_start(boB[:, n], ins.o_biases[n].partition_broadcast(P)).then_inc(small_in, 16)
                act.dma_start(lnwB[:, :], ins.lnw.partition_broadcast(P)).then_inc(small_in, 16)
                act.wait_ge(f_in, 32)
                for n in range(2):
                    if n:
                        act.wait_ge(abs_done, n)
                    nc.scalar.activation(junk[:, :], fnat[:, n], ACT.Abs, accum_out=asum[:, n:n + 1]).then_inc(abs_done, 1)
                for n in range(8):
                    act.wait_ge(w_T, n + 1)
                    nc.scalar.activation(WT[:, n, HI], bank[:, n, :].rearrange("p (k o) -> p k o", k=KT),
                                         ACT.Copy, scale=WS).then_inc(w_hi, 1)

            @block.gpsimd
            def _(pool):
                for t in (ident, ident16, identb):
                    nc.gpsimd.memset(t[:, :], 0.0).then_inc(zeroed, 1)
                nc.gpsimd.memset(ones[:, :], 1.0).then_inc(zeroed, 1)
                nc.gpsimd.memset(mhalf[:, :], -0.5).then_inc(zeroed, 1)
                pool.wait_ge(zeroed, 5)
                for t in (ident, ident16, identb):
                    nc.gpsimd.affine_select(out=t[:, :], in_=t[:, :], compare_op=ALU.not_equal, fill=1.0,
                                            base=0, pattern=[[-1, P]], channel_multiplier=1).then_inc(consts, 1)

            @block.vector
            def _(dve):
                dve.wait_ge(total_done, 1)
                nc.vector.tensor_scalar(thr[:, :], bank[:, 7, 0:2], 1.0 / (F * D), GAMMA_EPS, ALU.mult, ALU.add).then_inc(gamma_done, 1)
                dve.wait_ge(gamma_done, 1)
                nc.vector.tensor_scalar(nthr[:, :], thr[:, :], -0.5, None, ALU.mult).then_inc(thr_done, 1)
                dve.wait_ge(thr_done, 1)
                nc.vector.tensor_scalar(thr[:, :], thr[:, :], 0.5, None, ALU.mult).then_inc(thr_done, 1)
                dve.wait_ge(thr_done, 2)
                for n in range(2):
                    nc.vector.tensor_scalar(neg[:, n], fnat[:, n], nthr[:, n:n + 1], None, ALU.is_lt).then_inc(neg_done, 1)
                for n in range(2):
                    dve.wait_ge(neg_done, n + 1)
                    nc.vector.scalar_tensor_tensor(fnat[:, n], fnat[:, n], thr[:, n:n + 1], neg[:, n],
                                                   ALU.is_gt, ALU.subtract).then_inc(tern_done, 1)
                for n in range(8):
                    dve.wait_ge(w_hi, n + 1)
                    nc.vector.scalar_tensor_tensor(WT[:, n, LO].rearrange("p k o -> p (k o)"), bank[:, n, :], WS,
                                                   WT[:, n, HI].rearrange("p k o -> p (k o)"),
                                                   ALU.mult, ALU.subtract).then_inc(w_lo, 1)
                dve.wait_ge(small_in, 16 * NSMALL)
                nc.vector.tensor_scalar(bcol[:, :, :], bcol[:, :, :], WS, None, ALU.mult).then_inc(scaled, 1)
                for c in range(2 * KT):
                    last = nc.vector.tensor_copy(bvB[:, HI, c], bv_col[:, c:c + 1].broadcast_to([P, P]))
                last.then_inc(bv_split, 1)
                dve.wait_ge(bv_split, 1)
                for c in range(2 * KT):
                    last = nc.vector.tensor_tensor(bvB[:, LO, c], bv_col[:, c:c + 1].broadcast_to([P, P]), bvB[:, HI, c], ALU.subtract)
                last.then_inc(bv_split, 1)
                for t in range(FT):
                    last = nc.vector.tensor_copy(lnbB[:, t], lnb_col[:, t:t + 1].broadcast_to([P, P]))
                last.then_inc(lnb_done, 1)
                for kt in range(KT):
                    dve.wait_ge(f_T, kt + 1)
                    nc.vector.tensor_copy(wfcT[:, kt].rearrange("p (a h) -> p a h", a=2), bank[:, 2 * kt:2 * kt + 2, :]).then_inc(f_out, 1)
                dve.wait_ge(f_T, KT + 1)
                nc.vector.tensor_copy(wpT[:, :, :].rearrange("p (a t) d -> p a (t d)", a=4), bank[:, 4:8, :]).then_inc(f_out, 1)
                nc.vector.tensor_copy(wpT32[:, :, :].rearrange("p (a t) d -> p a (t d)", a=4), bank[:, 4:8, :]).then_inc(f_out, 1)
                dve.wait_ge(c2_mm, 1)
                nc.vector.tensor_copy(c2B[:, :], bank[:, 0, 0:D]).then_inc(c2_done, 1)
                dve.wait_ge(bo_mm, 1)
                nc.vector.scalar_tensor_tensor(boB[:, :, :].rearrange("p n d -> p (n d)"), bank[:, 2, :], 1.0 / WS,
                                               boB[:, :, :].rearrange("p n d -> p (n d)"), ALU.mult, ALU.add).then_inc(bo_done, 1)
                dve.wait_ge(mask_in, 16)
                nc.vector.tensor_copy(maskc[:, :], imask[:, :]).then_inc(m_done, 1)
                dve.wait_ge(m_done, 1)
                nc.vector.tensor_scalar(maskc[:, :], maskc[:, :], 0.0, None, ALU.is_equal).then_inc(mc_done, 1)
                dve.wait_ge(mc_done, 1)
                nc.vector.tensor_reduce(cntW[:, :], maskc[:, :], AX.X, ALU.add).then_inc(cnt_done, 1)
                for n in range(4):
                    nc.vector.tensor_scalar(maskB4[:, n], maskc[:, :], NEG, None, ALU.mult)
                dve.wait_ge(cnt_done, 1)
                nc.vector.tensor_scalar(mfloor[:, :], cntW[:, :], 0.0, NEG, ALU.is_le, ALU.mult).then_inc(cnt_done, 1)
                dve.wait_ge(cnt_done, 2)
                nc.vector.tensor_scalar(mfloor[:, :], mfloor[:, :], MASKED * HD ** 0.5 * SHIFT, None, ALU.add).then_inc(cnt_done, 1)
                nc.vector.tensor_scalar(cntW[:, :], cntW[:, :], WS, None, ALU.mult).then_inc(cnt_done, 1)
                dve.wait_ge(m_T, 1)
                nc.vector.tensor_copy(maskcT[:, :], bank[:, 1, 0:S]).then_inc(m_out, 1)
                for n in range(G):
                    nc.vector.tensor_scalar(maskBT4[:, n], bank[:, 1, 0:S], NEG, None, ALU.mult).then_inc(m_out, 1)

            @block.tensor
            def _(pe):
                pe.wait_ge(consts, 3)
                pe.wait_ge(abs_done, 2)
                nc.tensor.matmul(bank[:, 7, 0:2], ones[:, :], asum[:, :], start=True, stop=True).then_inc(total_done, 1)
                pe.wait_ge(gamma_done, 1)
                pe.wait_ge(w_in, 16 * 8)
                for n in range(8):
                    for mt in range(KT):
                        for kt in range(KT):
                            last = nc.tensor.transpose(bank[:, n, kt * D + mt * P:kt * D + (mt + 1) * P],
                                                       wnat[:, n, mt, kt * P:(kt + 1) * P], ident[:, :])
                    last.then_inc(w_T, 1)
                pe.wait_ge(w_lo, 8)
                pe.wait_ge(tern_done, 2)
                fc = fnat[:, 0].rearrange("p (t d) -> p t d", t=FT)
                pj = fnat[:, 1].rearrange("p (t h) -> p t h", t=KT)
                for kt in range(KT):
                    for t in range(FT):
                        last = nc.tensor.transpose(bank[:, 2 * kt + t // 4, (t % 4) * P:(t % 4 + 1) * P],
                                                   fc[:, t, kt * P:(kt + 1) * P], ident[:, :])
                    last.then_inc(f_T, 1)
                for t in range(FT):
                    for m in range(KT):
                        o = (t % 2) * D + m * P
                        last = nc.tensor.transpose(bank[:, 4 + t // 2, o:o + P], pj[:, m, t * P:(t + 1) * P], ident[:, :])
                last.then_inc(f_T, 1)
                pe.wait_ge(f_out, 4)
                pe.wait_ge(lnb_done, 1)
                for t in range(FT):
                    last = nc.tensor.matmul(bank[:, 0, 0:D], lnbB[:, t], wpT32[:, t], start=(t == 0), stop=(t == FT - 1))
                last.then_inc(c2_mm, 1)
                pe.wait_ge(bv_split, 2)
                for n, wo in enumerate((SO, XO)):
                    for m, (a, wp) in enumerate(SPLITS):
                        for kt in range(KT):
                            last = nc.tensor.matmul(bank[:, 2, n * D:(n + 1) * D], bvB[:, a, n * KT + kt], WT[:, wo, wp, kt],
                                                    start=(m == 0 and kt == 0), stop=(m == 2 and kt == KT - 1))
                last.then_inc(bo_mm, 1)
                pe.wait_ge(mc_done, 1)
                nc.tensor.transpose(bank[:, 1, 0:S], maskc[:, :], ident[:, :]).then_inc(m_T, 1)


class Chain:

    def __init__(self, name, sb, ps, sem, first_weight):
        n = name
        self.cross = name == "cross"
        self.wq, self.wk, self.wv, self.wo = range(first_weight, first_weight + 4)
        self.which = 1 if self.cross else 0
        self.src = sb(n + "_src", [P, G, D])
        self.stats = sb(n + "_stats", [P, G, 6])
        self.mv = sb(n + "_mv", [P, G, 2])
        self.ve = sb(n + "_ve", [P, G])
        self.rstd = sb(n + "_rstd", [P, G])
        self.xn = sb(n + "_xn", [P, G, D])
        self.xb = sb(n + "_xb", [P, G, D])
        self.xhl = sb(n + "_xhl", [P, 2, KT, T], F16)
        self.qk = sb(n + "_qk", [P, 4, KT, T], F16)
        self.stk = sb(n + "_stk", [P, 2, FT // 2, KT, T], F16)
        self.vals = sb(n + "_vals", [P, G, H, VW])
        self.prob = sb(n + "_prob", [P, 2, 4, T])
        self.oT = self.qk[:, :, :, :].rearrange("p a k t -> p (a k t)").bitcast(F32).rearrange("p (q t) -> p q t", q=QUADS)
        self.mx = sb(n + "_mx", [P, G * H])
        self.negm = sb(n + "_negm", [P, G * H], F16)
        self.negmT = sb(n + "_negmT", [H, T], F16)
        self.rec = sb(n + "_rec", [P, QUADS, G * 4])
        self.att = sb(n + "_att", [P, G, D])
        self.ahl = sb(n + "_ahl", [P, 2, KT, T], F16)
        self.bk = ps(n + "_bk", [P, 4, 512])
        if not self.cross:
            self.loaded = sem("self_loaded")
        self.stats_done = sem(n + "_stats_done")
        self.moments = sem(n + "_moments")
        self.var_ready = sem(n + "_var_ready")
        self.rstd_ready = sem(n + "_rstd_ready")
        self.xn_ready = sem(n + "_xn_ready")
        self.xb_ready = sem(n + "_xb_ready")
        self.xT_ready = sem(n + "_xT_ready")
        self.xhi_ready = sem(n + "_xhi_ready")
        self.xlo_ready = sem(n + "_xlo_ready")
        self.qk_mm = sem(n + "_qk_mm")
        self.qk_hi = sem(n + "_qk_hi")
        self.qk_lo = sem(n + "_qk_lo")
        self.v_mm = sem(n + "_v_mm")
        self.v_ready = sem(n + "_v_ready")
        self.stacked = sem(n + "_stacked")
        self.s_mm = sem(n + "_s_mm")
        self.max_done = sem(n + "_max_done")
        self.negm_ready = sem(n + "_negm_ready")
        self.mT_ready = sem(n + "_mT_ready")
        self.mT_out = sem(n + "_mT_out")
        self.m_in = sem(n + "_m_in")
        self.st_mm = sem(n + "_st_mm")
        self.exp_done = sem(n + "_exp_done")
        self.pv_done = sem(n + "_pv_done")
        self.o_out = sem(n + "_o_out")
        self.oT_ready = sem(n + "_oT_ready")
        if self.cross:
            self.den_ready = sem("cross_den_ready")
        self.rec_ready = sem(n + "_rec_ready")
        self.ao_ready = sem(n + "_ao_ready")
        self.aT_ready = sem(n + "_aT_ready")
        self.ahi_ready = sem(n + "_ahi_ready")
        self.alo_ready = sem(n + "_alo_ready")
        self.op_mm = sem(n + "_op_mm")
        self.y_ready = sem(n + "_y_ready")


def attention(nc, program, ins, sh, x2_dram):
    x_groups = ins.x.rearrange("(n b) s d -> n s b d", b=G)
    ctx_groups = ins.ctx.rearrange("(n b) s d -> n s b d", b=G)
    x2_groups = x2_dram.rearrange("(n b) s d -> n s b d", b=G)
    with ExitStack() as stack:
        sb, ps, sem = allocators(nc, stack, program)
        slf = Chain("self", sb, ps, sem, 0)
        crs = Chain("cross", sb, ps, sem, 4)
        cin = sb("ctx_in", [P, G, D])
        chl = sb("ctx_hl", [P, 2, KT, T], F16)
        earg = sb("earg", [P, G * H])
        ew = sb("ew", [P, G, H])
        ecnt = sb("ecnt", [P, G, H])
        ue = sb("ue", [P, G, D])
        nsum = sb("nsum", [P, QUADS, G, 4 * HD])
        dsum = sb("dsum", [P, QUADS, G * 4])
        yout = sb("yout", [P, G, D])
        held = sb("held_wait", [P, 1])
        primed = sem("primed")
        c_loaded, cT_ready, chi_ready, clo_ready = sem("c_loaded"), sem("cT_ready"), sem("chi_ready"), sem("clo_ready")
        earg_ready, ew_ready, ecnt_ready = sem("earg_ready"), sem("ew_ready"), sem("ecnt_ready")
        u_mm, ue_ready, stored = sem("u_mm"), sem("ue_ready"), sem("stored")

        def present(g):
            return g if not isinstance(g, int) or 0 <= g < NG else None

        def step(slot, i):
            slot(crs, slf, present(i - 1), present(i), present(i + 1), present(i))
            slot(slf, crs, present(i + 1), present(i - 1), present(i), present(i + 2))

        def steps(engine, slot):
            for i in range(-2, 2):
                step(slot, i)
            with engine.Fori(2, NG - 2) as i:
                step(slot, i)
            for i in range(NG - 2, NG + 1):
                step(slot, i)


        def out_bank(ch, qd):
            return ch.bk[:, 2, :] if qd == QUADS - 1 else (slf if ch.cross else crs).bk[:, 2 + qd % 2, :]

        def turned_bank(ch, qd):
            return ch.bk[:, (3, 1)[qd - 2], :] if qd > 1 else (slf if ch.cross else crs).bk[:, qd, :]


        def stack_rows(sp, ch, g):
            sp.wait_ge(ch.qk_lo, 4 * g + 4)
            for j in range(FT):
                rows, to, p = slice(HD * j, HD * j + HD), HALF * (j % 2), j // 2
                for k, parts in enumerate((slice(1, 3), slice(0, 3, 2), slice(1, 4, 2))):
                    sp.dma_start(ch.stk[to + HD * k:to + HD * k + HD, :, p], ch.qk[rows, parts]).then_inc(ch.stacked, 16)

        def sp_slot(sp, y, x, att, tail, proj, norm):
            if x.cross and tail is not None:
                x2_group = x2_groups[tail]
                sp.wait_ge(crs.y_ready, 2 * tail + 2)
                sp.dma_start(x2_group, yout[:, :, :]).then_inc(stored, 16)
            if proj is not None:
                if present(proj + 1) is not None:
                    if x.cross:
                        ctx_group = ctx_groups[proj + 1]
                        sp.wait_ge(cT_ready, proj + 1)
                        sp.dma_start(cin[:, :, :], ctx_group).then_inc(c_loaded, 16)
                    else:
                        x_group = x_groups[proj + 1]
                        sp.wait_ge(slf.xb_ready, proj + 1)
                        sp.dma_start(slf.src[:, :, :], x_group).then_inc(slf.loaded, 16)
                stack_rows(sp, x, proj)


        def pool_slot(pool, y, x, att, tail, proj, norm):
            if proj is not None:
                pool.wait_ge(x.xn_ready, proj + 1)
                wait(pool, x.y_ready, 2 * proj)
                nc.gpsimd.tensor_tensor(x.xb[:, :, :], x.src[:, :, :], sh.boB[:, x.which:x.which + 1, :].broadcast_to([P, G, D]),
                                        ALU.add).then_inc(x.xb_ready, 1)
            if norm is not None:
                pool.wait_ge(y.var_ready, norm + 1)
                wait(pool, y.xn_ready, norm)
                nc.gpsimd.tensor_tensor(y.rstd[:, :], y.ve[:, :], sh.mhalf[:, :], ALU.pow).then_inc(y.rstd_ready, 1)


        def act_qk(act, ch, g, n):
            act.wait_ge(ch.qk_mm, 4 * g + n + 1)
            if n == 0:
                wait(act, ch.stacked, 16 * STACK_DMAS * g)
            act.activation(ch.qk[:, 1 + n // 2, n % 2], ch.bk[:, n, :], ACT.Identity,
                           bias=sh.bcol[:, 2 * ch.which + n // 2, n % 2:n % 2 + 1]).then_inc(ch.qk_hi, 1)

        def act_slot(y, x, att, tail, proj, norm):
            act = nc.scalar
            if tail is not None:
                act.wait_ge(x.aT_ready, tail + 1)
                act.activation(x.ahl[:, HI], x.bk[:, 0:2, :], ACT.Copy).then_inc(x.ahi_ready, 1)
            if proj is not None:
                act.wait_ge(x.xT_ready, proj + 1)
                act.activation(x.xhl[:, HI], x.bk[:, 0:2, :], ACT.Copy).then_inc(x.xhi_ready, 1)
                act_qk(act, x, proj, 0)
                if x.cross:
                    act.wait_ge(cT_ready, proj + 1)
                    act.activation(chl[:, HI], x.bk[:, 2:4, :], ACT.Copy).then_inc(chi_ready, 1)
                act_qk(act, x, proj, 1)
            if att is not None:
                act.wait_ge(y.mT_ready, att + 1)
                wait(act, y.m_in, 32 * att)
                act.activation(y.negmT[:, :], y.bk[0:H, 0, 0:T // 2].bitcast(F16), ACT.Copy).then_inc(y.mT_out, 1)
                act.wait_ge(y.mT_out, att + 1)
                for r in range(2):
                    act.dma_start(y.stk[HALF * r + STACK:HALF * (r + 1), 0].rearrange("p a k t -> p (a k) t"),
                                  y.negmT[:, :].unsqueeze(1).broadcast_to([H, PAIRS, T])).then_inc(y.m_in, 16)
                if y.cross:
                    act.wait_ge(earg_ready, att + 1)
                    act.activation(ew[:, :, :].rearrange("p b h -> p (b h)"), earg[:, :], ACT.Exp, scale=HD ** -0.5).then_inc(ew_ready, 1)
            if proj is not None:
                for n in (2, 3):
                    act_qk(act, x, proj, n)
                for n in range(2):
                    act.wait_ge(x.v_mm, 2 * proj + n + 1)
                    act.activation(x.vals[:, 2 * n:2 * n + 2, :, 0:HD].rearrange("p b h d -> p (b h) d"),
                                   x.bk[:, n, :].rearrange("p (a d) -> p a d", d=HD), ACT.Copy).then_inc(x.v_ready, 1)
            if att is not None:
                for n in range(H):
                    qd = n // 4
                    if n % 4 == 0 and qd > 1:
                        act.wait_ge(y.pv_done, 4 * att + qd - 1)
                    act.wait_ge(y.st_mm, 16 * att + n + 1)
                    act.activation(y.prob[:, qd % 2, n % 4], y.bk[:, n % 4, :], ACT.Exp, scale=EXP_SCALE).then_inc(y.exp_done, 1)


        def dve_qk(dve, ch, g, n):
            dve.wait_ge(ch.qk_hi, 4 * g + n + 1)
            dve.scalar_tensor_tensor(ch.qk[:, 3 * (n // 2), n % 2], ch.bk[:, n, :],
                                     sh.bcol[:, 2 * ch.which + n // 2, n % 2:n % 2 + 1],
                                     ch.qk[:, 1 + n // 2, n % 2], ALU.add, ALU.subtract).then_inc(ch.qk_lo, 1)

        def dve_max(dve, ch, g, m):
            dve.wait_ge(ch.s_mm, 8 * g + m + 1)
            o = 2 * (m % 2)
            dve.tensor_reduce(ch.mx[:, 8 * m:8 * m + 8].rearrange("p (j r) -> p r j", r=2),
                              ch.bk[:, o:o + 2, :].rearrange("p r (j k) -> p r j k", j=4), AX.X, ALU.max).then_inc(ch.max_done, 1)

        def dve_normalise(dve, ch, g, qd):
            dve.wait_ge(ch.oT_ready, 4 * g + qd + 1)
            bank = turned_bank(ch, qd)
            o = bank.rearrange("p (b h c) -> p b h c", b=G, h=4)
            num, den = o[:, :, :, 0:HD], bank[:, HD::VW]
            if ch.cross:
                if qd == 0:
                    dve.wait_ge(ue_ready, 2 * g + 2)
                    dve.wait_ge(ecnt_ready, g + 1)
                summed = nsum[:, qd].rearrange("p b (h d) -> p b h d", d=HD)
                dve.tensor_tensor(summed, num, ue[:, :, qd * 4 * HD:(qd + 1) * 4 * HD].rearrange("p b (h d) -> p b h d", d=HD), ALU.add)
                dve.tensor_tensor(dsum[:, qd].rearrange("p (b h) -> p b h", b=G), o[:, :, :, HD],
                                  ecnt[:, :, 4 * qd:4 * qd + 4], ALU.add).then_inc(ch.den_ready, 1)
                dve.wait_ge(ch.den_ready, 4 * g + qd + 1)
                num, den = summed, dsum[:, qd]
            dve.reciprocal(ch.rec[:, qd], den).then_inc(ch.rec_ready, 1)
            dve.wait_ge(ch.rec_ready, 4 * g + qd + 1)
            dve.tensor_tensor(ch.att[:, :, qd * 4 * HD:(qd + 1) * 4 * HD].rearrange("p b (h d) -> p b h d", d=HD), num,
                              ch.rec[:, qd].rearrange("p (b h) -> p b h", b=G).unsqueeze(3).broadcast_to([P, G, 4, HD]),
                              ALU.mult).then_inc(ch.ao_ready, 1)

        def dve_residual(dve, ch, g, n):
            dve.wait_ge(ch.op_mm, 2 * g + n + 1)
            if n == 0:
                dve.wait_ge(ch.xb_ready, g + 1)
                if ch.cross:
                    wait(dve, stored, 16 * g)
                else:
                    wait(dve, crs.xb_ready, g)
            y = yout if ch.cross else crs.src
            dve.scalar_tensor_tensor(y[:, 2 * n:2 * n + 2].rearrange("p b d -> p (b d)"), ch.bk[:, 2 + n, :], 1.0 / WS,
                                     ch.xb[:, 2 * n:2 * n + 2].rearrange("p b d -> p (b d)"),
                                     ALU.mult, ALU.add).then_inc(ch.y_ready, 1)

        def dve_slot(y, x, att, tail, proj, norm):
            dve = nc.vector

            def maxima(*eights):
                if att is not None:
                    for m in eights:
                        dve_max(dve, y, att, m)

            if x.cross:
                maxima(0)
            if tail is not None:
                dve_normalise(dve, x, tail, QUADS - 1)
            if not x.cross:
                maxima(0)
            maxima(1, 2)
            if tail is not None:
                dve.wait_ge(x.ahi_ready, tail + 1)
                dve.tensor_tensor(x.ahl[:, LO], x.bk[:, 0:2, :], x.ahl[:, HI], ALU.subtract).then_inc(x.alo_ready, 1)
            maxima(3, 4)
            if proj is not None:
                dve.wait_ge(x.xhi_ready, proj + 1)
                dve.tensor_tensor(x.xhl[:, LO], x.bk[:, 0:2, :], x.xhl[:, HI], ALU.subtract).then_inc(x.xlo_ready, 1)
            for n in range(2):
                maxima(5 + n)
                if tail is not None:
                    dve_residual(dve, x, tail, n)
            maxima(7)
            if att is not None:
                dve.wait_ge(y.max_done, 8 * att + 8)
                if y.cross:
                    dve.tensor_scalar(y.negm[:, :], y.mx[:, :], sh.mfloor[:, :], -1.0 / SHIFT, ALU.max, ALU.mult).then_inc(y.negm_ready, 1)
                    dve.wait_ge(y.negm_ready, att + 1)
                    dve.tensor_scalar(earg[:, :], y.negm[:, :], 0.0, MASKED * HD ** 0.5, ALU.min, ALU.add).then_inc(earg_ready, 1)
                else:
                    dve.tensor_scalar(y.negm[:, :], y.mx[:, :], -1.0 / SHIFT, None, ALU.mult).then_inc(y.negm_ready, 1)
            if proj is not None:
                dve_qk(dve, x, proj, 0)
                if x.cross:
                    dve.wait_ge(chi_ready, proj + 1)
                    dve.tensor_tensor(chl[:, LO], x.bk[:, 2:4, :], chl[:, HI], ALU.subtract).then_inc(clo_ready, 1)
                for n in (1, 2, 3):
                    dve_qk(dve, x, proj, n)
            if norm is not None:
                if y.cross:
                    dve.wait_ge(slf.y_ready, 2 * norm + 2)
                else:
                    dve.wait_ge(slf.loaded, 16 * norm + 16)
                for b in range(G):
                    dve.bn_stats(y.stats[:, b], y.src[:, b]).then_inc(y.stats_done, 1)
                dve.wait_ge(y.stats_done, 4 * norm + 4)
                dve.memset(held[:, :], 0.0)
                for b in range(G):
                    last = dve.bn_aggr(y.mv[:, b], y.stats[:, b])
                last.then_inc(y.moments, 1)
                dve.wait_ge(y.moments, norm + 1)
                dve.tensor_scalar(y.ve[:, :], y.mv[:, :, 1], LN_EPS, None, ALU.add).then_inc(y.var_ready, 1)
            if att is not None and y.cross:
                dve.wait_ge(ew_ready, att + 1)
                dve.tensor_scalar(ecnt[:, :, :], ew[:, :, :], sh.cntW[:, :], None, ALU.mult).then_inc(ecnt_ready, 1)
                for n in range(2):
                    dve.wait_ge(u_mm, 2 * att + n + 1)
                    dve.tensor_tensor(ue[:, 2 * n:2 * n + 2].rearrange("p b (h d) -> p (b h) d", d=HD),
                                      y.bk[:, (1, 3)[n], :].rearrange("p (a d) -> p a d", d=HD),
                                      ew[:, 2 * n:2 * n + 2].rearrange("p b h -> p (b h)").unsqueeze(2).broadcast_to([P, 2 * H, HD]),
                                      ALU.mult).then_inc(ue_ready, 1)
            if norm is not None:
                dve.wait_ge(y.rstd_ready, norm + 1)
                for b in range(G):
                    last = dve.tensor_scalar(y.xn[:, b], y.src[:, b], y.mv[:, b, 0:1], y.rstd[:, b:b + 1],
                                             ALU.subtract, ALU.mult)
                last.then_inc(y.xn_ready, 1)
            if att is not None:
                for qd in range(QUADS):
                    dve.wait_ge(y.pv_done, 4 * att + qd + 1)
                    dve.tensor_copy(y.oT[:, qd], out_bank(y, qd)).then_inc(y.o_out, 1)
                    if qd:
                        dve_normalise(dve, y, att, qd - 1)


        def tile_product(ch, bank, w, tile, moving):
            for n, (a, wp) in enumerate(SPLITS):
                for kt in range(KT):
                    last = nc.tensor.matmul(ch.bk[:, bank, :], sh.WT[:, w, wp, kt, tile * P:(tile + 1) * P], moving[:, a, kt, :],
                                            start=(n == 0 and kt == 0), stop=(n == 2 and kt == KT - 1))
            return last

        def token_product(ch, bank, w, b, tokens):
            for n, (a, wp) in enumerate(SPLITS):
                for kt in range(KT):
                    last = nc.tensor.matmul(ch.bk[:, bank, (b % 2) * D:(b % 2 + 1) * D], tokens[:, a, kt, b * S:(b + 1) * S],
                                            sh.WT[:, w, wp, kt, :], start=(n == 0 and kt == 0), stop=(n == 2 and kt == KT - 1))
            return last

        def turn(ch, bank, src):
            for kt in range(KT):
                for b in range(G):
                    last = nc.tensor.transpose(ch.bk[:, bank + kt, b * S:(b + 1) * S], src[:, b, kt * P:(kt + 1) * P], sh.ident[:, :])
            return last

        def pe_scores(pe, ch, g, m):
            b, eight = divmod(m, 2)
            if m == 0:
                pe.wait_ge(ch.stacked, 16 * STACK_DMAS * (g + 1))
                pe.wait_ge(ch.v_ready, 2 * g + 2)
            if m > 1:
                pe.wait_ge(ch.max_done, 8 * g + m - 1)
            if ch.cross:
                for r in range(2):
                    pe.matmul(ch.bk[:, 2 * (m % 2) + r, :], sh.identb[:, :], sh.maskB4[:, :, :], start=True, stop=False, skip_group_check=True)
            for j in range(4):
                for r in range(2):
                    rows = slice(HALF * r, HALF * r + STACK)
                    last = pe.matmul(ch.bk[:, 2 * (m % 2) + r, j * S:(j + 1) * S], ch.stk[rows, 0, j, eight, b * S:(b + 1) * S],
                                     ch.stk[rows, 1, j, eight, b * S:(b + 1) * S], start=not ch.cross, stop=True, skip_group_check=True)
            last.then_inc(ch.s_mm, 1)

        def pe_shifted(pe, ch, g, n):
            if n == 0:
                pe.wait_ge(ch.m_in, 32 * (g + 1))
            if n in (1, 3) and ch.cross:
                pe.wait_ge(ue_ready, 2 * g + (n + 1) // 2)
            if n > 3:
                pe.wait_ge(ch.exp_done, 16 * g + n - 3)
            if ch.cross:
                pe.matmul(ch.bk[:, n % 4, :], sh.identb[:, :], sh.maskBT4[:, :, :], start=True, stop=False, skip_group_check=True)
            rows = slice(HALF * (n % 2), HALF * (n % 2 + 1))
            for b in range(G):
                last = pe.matmul(ch.bk[:, n % 4, b * S:(b + 1) * S], ch.stk[rows, 1, n // 2 % 4, n // 8, b * S:(b + 1) * S],
                                 ch.stk[rows, 0, n // 2 % 4, n // 8, b * S:(b + 1) * S], start=not ch.cross, stop=True, skip_group_check=True)
            last.then_inc(ch.st_mm, 1)

        def pe_values(pe, ch, g, qd):
            pe.wait_ge(ch.exp_done, 16 * g + 4 * qd + 4)
            if qd == 2:
                pe.wait_ge(ch.o_out, 4 * g + 1)
            for b in range(G):
                for jq in range(4):
                    last = pe.matmul(out_bank(ch, qd)[32 * jq:32 * jq + VW, b * S:(b + 1) * S], ch.vals[:, b, 4 * qd + jq, :],
                                     ch.prob[:, qd % 2, jq, b * S:(b + 1) * S], start=True, stop=True, skip_group_check=True)
            last.then_inc(ch.pv_done, 1)

        def pe_turn_outputs(pe, ch, g, qd):
            pe.wait_ge(ch.o_out, 4 * g + qd + 1)
            for b in range(G):
                last = pe.transpose(turned_bank(ch, qd)[:, b * S:(b + 1) * S], ch.oT[:, qd, b * S:(b + 1) * S], sh.ident[:, :])
            last.then_inc(ch.oT_ready, 1)

        def pe_slot(y, x, att, tail, proj, norm):
            pe = nc.tensor
            other = chl if x.cross else x.xhl

            def scores(*eights):
                if att is not None:
                    for m in eights:
                        pe_scores(pe, y, att, m)

            if x.cross:
                scores(0, 1)
            if tail is not None:
                pe_turn_outputs(pe, x, tail, QUADS - 1)
            if x.cross:
                scores(2)
            if tail is not None:
                pe.wait_ge(x.ao_ready, 4 * tail + 4)
                turn(x, 0, x.att).then_inc(x.aT_ready, 1)
            if not x.cross:
                scores(0, 1, 2)
            scores(3, 4)
            if proj is not None:
                pe.wait_ge(x.xn_ready, proj + 1)
                if tail is not None:
                    pe.wait_ge(x.alo_ready, tail + 1)
                turn(x, 0, x.xn).then_inc(x.xT_ready, 1)
            scores(5)
            for n in range(2):
                if tail is not None:
                    if n == 0:
                        pe.wait_ge(x.alo_ready, tail + 1)
                    for b in (2 * n, 2 * n + 1):
                        last = token_product(x, 2 + n, x.wo, b, x.ahl)
                    last.then_inc(x.op_mm, 1)
                if n == 0:
                    scores(6)
            if proj is not None:
                pe.wait_ge(x.xlo_ready, proj + 1)
                tile_product(x, 0, x.wq, 0, x.xhl).then_inc(x.qk_mm, 1)
            scores(7)
            if proj is not None and x.cross:
                pe.wait_ge(c_loaded, 16 * proj + 16)
                if tail is not None:
                    pe.wait_ge(x.y_ready, 2 * tail + 2)
                turn(x, 2, cin).then_inc(cT_ready, 1)
            if proj is not None:
                tile_product(x, 1, x.wq, 1, x.xhl).then_inc(x.qk_mm, 1)
            if att is not None:
                pe.wait_ge(y.negm_ready, att + 1)
                for b in range(G):
                    last = pe.transpose(y.bk[0:H, 0, b * S // 2:(b + 1) * S // 2].bitcast(F16), y.negm[:, b * H:(b + 1) * H], sh.ident16[:, :])
                last.then_inc(y.mT_ready, 1)
                if y.cross:
                    for b in range(G):
                        last = pe.matmul(y.bk[:, (1, 3)[b // 2], (b % 2) * D:(b % 2 + 1) * D], sh.maskcT[:, :],
                                         y.vals[:, b, :, 0:HD], start=True, stop=True)
                        if b % 2:
                            last.then_inc(u_mm, 1)
            if proj is not None:
                if x.cross:
                    pe.wait_ge(clo_ready, proj + 1)
                elif tail is not None:
                    pe.wait_ge(x.y_ready, 2 * tail + 2)
                for n in (2, 3):
                    tile_product(x, n, x.wk, n - 2, other).then_inc(x.qk_mm, 1)
                for n in range(2):
                    pe.wait_ge(x.qk_lo, 4 * proj + n + 1)
                    for b in (2 * n, 2 * n + 1):
                        last = token_product(x, n, x.wv, b, other)
                    last.then_inc(x.v_mm, 1)
            if att is not None:
                for qd in range(QUADS):
                    pe_shifted(pe, y, att, 4 * qd)
                    pe_shifted(pe, y, att, 4 * qd + 1)
                    if qd == 1:
                        if proj is not None:
                            pe.wait_ge(x.qk_lo, 4 * proj + 4)
                            pe.wait_ge(x.v_ready, 2 * proj + 2)
                        elif tail is not None:
                            pe.wait_ge(x.y_ready, 2 * tail + 2)
                    if qd > 0:
                        pe_values(pe, y, att, qd - 1)
                    pe_shifted(pe, y, att, 4 * qd + 2)
                    if qd > 1:
                        pe_turn_outputs(pe, y, att, qd - 2)
                    pe_shifted(pe, y, att, 4 * qd + 3)
                pe_values(pe, y, att, QUADS - 1)
                pe_turn_outputs(pe, y, att, QUADS - 2)
                pe.wait_ge(y.ao_ready, 4 * att + 2)

        with nc.Block() as block:
            @block.sync
            def _(sp):
                sp.dma_start(slf.src[:, :, :], x_groups[0]).then_inc(slf.loaded, 16)
                sp.dma_start(cin[:, :, :], ctx_groups[0]).then_inc(c_loaded, 16)
                sp.wait_ge(primed, 8)
                steps(sp, lambda *a: sp_slot(sp, *a))
                sp.wait_ge(stored, 16 * NG)

            @block.gpsimd
            def _(pool):
                for ch in (slf, crs):
                    nc.gpsimd.memset(ch.vals[:, :, :, :], 0.0).then_inc(primed, 1)
                    nc.gpsimd.memset(ch.stk[:, 1], 0.0).then_inc(primed, 1)
                for r in range(2):
                    pool.wait_ge(primed, 4 + 2 * r)
                    for ch in (slf, crs):
                        nc.gpsimd.affine_select(out=ch.stk[:, 1], in_=ch.stk[:, 1], compare_op=ALU.not_equal, fill=SHIFT,
                                                base=-(HALF * r + STACK + r), pattern=[[-2, FT // 2], [-FT, KT], [0, T]],
                                                channel_multiplier=1).then_inc(primed, 1)
                for ch in (slf, crs):
                    nc.gpsimd.memset(ch.vals[:, :, :, HD:HD + 1], WS).then_inc(primed, 1)
                steps(pool, lambda *a: pool_slot(pool, *a))

            @block.scalar
            def _(act):
                act.wait_ge(primed, 10)
                steps(act, act_slot)

            @block.vector
            def _(dve):
                steps(dve, dve_slot)

            @block.tensor
            def _(pe):
                steps(pe, pe_slot)


class Lane:

    def __init__(self, n, sb, ps, sem):
        self.src = sb(n + "_src", [P, G, D])
        self.stats = sb(n + "_stats", [P, G, 6])
        self.mv = sb(n + "_mv", [P, G, 2])
        self.ve = sb(n + "_ve", [P, G])
        self.rstd = sb(n + "_rstd", [P, G])
        self.xn = sb(n + "_xn", [P, G, D])
        self.xc = sb(n + "_xc", [P, G, D])
        self.xhl = sb(n + "_xhl", [P, 2, KT, T], F16)
        self.hid = sb(n + "_hid", [P, 2, F])
        self.hstats = sb(n + "_hstats", [P, G, 2, 6])
        self.hmv = sb(n + "_hmv", [P, G, 2])
        self.hve = sb(n + "_hve", [P, G])
        self.hrstd = sb(n + "_hrstd", [P, G])
        self.cen = sb(n + "_cen", [P, 2, F])
        self.chl = sb(n + "_chl", [P, 2, 2, FT, S], F16)
        self.y = sb(n + "_y", [P, G, D])
        self.bk = ps(n + "_bk", [P, 4, 512])
        self.loaded = sem(n + "_loaded")
        self.stats_done = sem(n + "_stats_done")
        self.moments = sem(n + "_moments")
        self.var_ready = sem(n + "_var_ready")
        self.rstd_ready = sem(n + "_rstd_ready")
        self.xn_ready = sem(n + "_xn_ready")
        self.xc_ready = sem(n + "_xc_ready")
        self.xT_ready = sem(n + "_xT_ready")
        self.xhi_ready = sem(n + "_xhi_ready")
        self.xlo_ready = sem(n + "_xlo_ready")
        self.h_mm = sem(n + "_h_mm")
        self.hid_ready = sem(n + "_hid_ready")
        self.hstats_done = sem(n + "_hstats_done")
        self.hmv_ready = sem(n + "_hmv_ready")
        self.cen_ready = sem(n + "_cen_ready")
        self.hve_ready = sem(n + "_hve_ready")
        self.hrstd_ready = sem(n + "_hrstd_ready")
        self.cT_ready = sem(n + "_cT_ready")
        self.chi_ready = sem(n + "_chi_ready")
        self.clo_ready = sem(n + "_clo_ready")
        self.y_mm = sem(n + "_y_mm")
        self.y_ready = sem(n + "_y_ready")
        self.stored = sem(n + "_stored")


def ffn(nc, program, sh, x2_dram, out):
    x2_groups = x2_dram.rearrange("(n b) s d -> n s b d", b=G)
    out_groups = out.rearrange("(n b) s d -> n s b d", b=G)
    with ExitStack() as stack:
        sb, ps, sem = allocators(nc, stack, program)
        lanes = [Lane("even", sb, ps, sem), Lane("odd", sb, ps, sem)]
        STEPS = NG // 2
        held = sb("held", [P, 1])

        def sp_load(sp, i):
            for c, ln in enumerate(lanes):
                x2_group = x2_groups[2 * i + c]
                wait(sp, ln.xn_ready, i)
                wait(sp, ln.xc_ready, i)
                sp.dma_start(ln.src[:, :, :], x2_group).then_inc(ln.loaded, 16)

        def sp_store(sp, i):
            for c, ln in enumerate(lanes):
                out_group = out_groups[2 * i + c]
                sp.wait_ge(ln.y_ready, 4 * i + 4)
                sp.dma_start(out_group, ln.y[:, :, :]).then_inc(ln.stored, 16)

        def pool_step(pool, i):
            for ln in lanes:
                pool.wait_ge(ln.var_ready, i + 1)
                wait(pool, ln.xn_ready, i)
                nc.gpsimd.tensor_tensor(ln.rstd[:, :], ln.ve[:, :], sh.mhalf[:, :], ALU.pow).then_inc(ln.rstd_ready, 1)
            for ln in lanes:
                pool.wait_ge(ln.loaded, 16 * i + 16)
                wait(pool, ln.y_ready, 4 * i)
                nc.gpsimd.tensor_tensor(ln.xc[:, :, :], ln.src[:, :, :], sh.c2B[:, :].unsqueeze(1).broadcast_to([P, G, D]),
                                        ALU.add).then_inc(ln.xc_ready, 1)
            for b in range(G):
                for ln in lanes:
                    pool.wait_ge(ln.hve_ready, 4 * i + b + 1)
                    nc.gpsimd.tensor_tensor(ln.hrstd[:, b:b + 1], ln.hve[:, b:b + 1], sh.mhalf[:, 0:1], ALU.pow).then_inc(ln.hrstd_ready, 1)

        def act_step(i):
            act = nc.scalar
            for ln in lanes:
                act.wait_ge(ln.xT_ready, i + 1)
                act.activation(ln.xhl[:, HI], ln.bk[:, 0:2, :], ACT.Copy).then_inc(ln.xhi_ready, 1)
            for b in range(G + 1):
                for ln in lanes:
                    if b < G:
                        o = 2 * (b % 2)
                        act.wait_ge(ln.h_mm, 4 * i + b + 1)
                        wait(act, ln.cT_ready, 4 * i + b - 1)
                        act.activation(ln.hid[:, b % 2].rearrange("p (a h) -> p a h", a=2), ln.bk[:, o:o + 2, :], ACT.Gelu).then_inc(ln.hid_ready, 1)
                    if b:
                        c = b - 1
                        o = 2 * (c % 2)
                        act.wait_ge(ln.cT_ready, 4 * i + c + 1)
                        wait(act, ln.y_mm, 4 * i + c - 1)
                        act.activation(ln.chl[:, c % 2, HI].rearrange("p (a t) s -> p a (t s)", a=2), ln.bk[:, o:o + 2, :], ACT.Copy).then_inc(ln.chi_ready, 1)

        def dve_step(i):
            dve = nc.vector
            for n, ln in enumerate(lanes):
                dve.wait_ge(ln.loaded, 16 * i + 16)
                for b in range(G):
                    if n and b == G - 1:
                        dve.wait_ge(lanes[0].stats_done, 4 * i + 4)
                    dve.bn_stats(ln.stats[:, b], ln.src[:, b]).then_inc(ln.stats_done, 1)
            for n, ln in enumerate(lanes):
                for b in range(G):
                    last = dve.bn_aggr(ln.mv[:, b], ln.stats[:, b])
                last.then_inc(ln.moments, 1)
                if n == 0:
                    dve.wait_ge(lanes[1].stats_done, 4 * i + 4)
                dve.wait_ge(ln.moments, i + 1)
                dve.tensor_scalar(ln.ve[:, :], ln.mv[:, :, 1], LN_EPS, None, ALU.add).then_inc(ln.var_ready, 1)
            for ln in lanes:
                dve.wait_ge(ln.rstd_ready, i + 1)
                for b in range(G):
                    last = dve.tensor_scalar(ln.xn[:, b], ln.src[:, b], ln.mv[:, b, 0:1], ln.rstd[:, b:b + 1],
                                             ALU.subtract, ALU.mult)
                last.then_inc(ln.xn_ready, 1)
            for ln in lanes:
                dve.wait_ge(ln.xhi_ready, i + 1)
                dve.tensor_tensor(ln.xhl[:, LO], ln.bk[:, 0:2, :], ln.xhl[:, HI], ALU.subtract).then_inc(ln.xlo_ready, 1)
            for b in range(G + 2):
                for ln in lanes:
                    if b > 1:
                        c = b - 2
                        dve.wait_ge(ln.y_mm, 4 * i + c + 1)
                        dve.wait_ge(ln.hrstd_ready, 4 * i + c + 1)
                        if c == 0:
                            dve.wait_ge(ln.xc_ready, i + 1)
                            wait(dve, ln.stored, 16 * i)
                        dve.scalar_tensor_tensor(ln.y[:, c], ln.bk[:, 2 * (c % 2), 0:D], ln.hrstd[:, c:c + 1], ln.xc[:, c],
                                                 ALU.mult, ALU.add).then_inc(ln.y_ready, 1)
                    if b < G:
                        m = 4 * i + b + 1
                        dve.wait_ge(ln.hid_ready, m)
                        for a in range(2):
                            last = dve.bn_stats(ln.hstats[:, b, a], ln.hid[:, b % 2, a * (F // 2):(a + 1) * (F // 2)])
                        last.then_inc(ln.hstats_done, 1)
                        dve.wait_ge(ln.hstats_done, m)
                        dve.memset(held[:, :], 0.0)
                        dve.bn_aggr(ln.hmv[:, b], ln.hstats[:, b].rearrange("p a s -> p (a s)")).then_inc(ln.hmv_ready, 1)
                        dve.wait_ge(ln.hmv_ready, m)
                        dve.scalar_tensor_tensor(ln.cen[:, b % 2], ln.hid[:, b % 2], ln.hmv[:, b, 0:1], sh.lnwB[:, :],
                                                 ALU.subtract, ALU.mult).then_inc(ln.cen_ready, 1)
                        dve.tensor_scalar(ln.hve[:, b:b + 1], ln.hmv[:, b, 1:2], LN_EPS, None, ALU.add).then_inc(ln.hve_ready, 1)
                    if 0 < b <= G:
                        c = b - 1
                        dve.wait_ge(ln.chi_ready, 4 * i + c + 1)
                        dve.tensor_tensor(ln.chl[:, c % 2, LO].rearrange("p (a t) s -> p a (t s)", a=2), ln.bk[:, 2 * (c % 2):2 * (c % 2) + 2, :],
                                          ln.chl[:, c % 2, HI].rearrange("p (a t) s -> p a (t s)", a=2), ALU.subtract).then_inc(ln.clo_ready, 1)

        def pe_step(i):
            pe = nc.tensor
            for ln in lanes:
                pe.wait_ge(ln.xn_ready, i + 1)
                wait(pe, ln.y_ready, 4 * i)
                for kt in range(KT):
                    for b in range(G):
                        last = pe.transpose(ln.bk[:, kt, b * S:(b + 1) * S], ln.xn[:, b, kt * P:(kt + 1) * P], sh.ident[:, :])
                last.then_inc(ln.xT_ready, 1)
            for b in range(G + 2):
                for ln in lanes:
                    if b > 1:
                        c = b - 2
                        pe.wait_ge(ln.clo_ready, 4 * i + c + 1)
                        for part in (HI, LO):
                            for t in range(FT):
                                last = pe.matmul(ln.bk[:, 2 * (c % 2), 0:D], ln.chl[:, c % 2, part, t], sh.wpT[:, t],
                                                 start=(part == HI and t == 0), stop=(part == LO and t == FT - 1))
                        last.then_inc(ln.y_mm, 1)
                    if b < G:
                        if b == 0:
                            pe.wait_ge(ln.xlo_ready, i + 1)
                        if b > 1:
                            pe.wait_ge(ln.y_ready, 4 * i + b - 1)
                        for a in range(2):
                            for part in (HI, LO):
                                for kt in range(KT):
                                    last = pe.matmul(ln.bk[:, 2 * (b % 2) + a, :], ln.xhl[:, part, kt, b * S:(b + 1) * S],
                                                     sh.wfcT[:, kt, a * 512:(a + 1) * 512],
                                                     start=(part == HI and kt == 0), stop=(part == LO and kt == KT - 1))
                        last.then_inc(ln.h_mm, 1)
                    if 0 < b <= G:
                        c = b - 1
                        pe.wait_ge(ln.cen_ready, 4 * i + c + 1)
                        for t in range(FT):
                            last = pe.transpose(ln.bk[:, 2 * (c % 2) + t // 4, (t % 4) * S:(t % 4 + 1) * S],
                                                ln.cen[:, c % 2, t * P:(t + 1) * P], sh.ident[:, :])
                        last.then_inc(ln.cT_ready, 1)

        with nc.Block() as block:
            @block.sync
            def _(sp):
                sp_load(sp, 0)
                sp_load(sp, 1)
                sp_store(sp, 0)
                with sp.Fori(1, STEPS - 1) as i:
                    sp_load(sp, i + 1)
                    sp_store(sp, i)
                sp_store(sp, STEPS - 1)
                for ln in lanes:
                    sp.wait_ge(ln.stored, 16 * STEPS)

            @block.gpsimd
            def _(pool):
                pool_step(pool, 0)
                with pool.Fori(1, STEPS) as i:
                    pool_step(pool, i)

            @block.scalar
            def _(act):
                act_step(0)
                with act.Fori(1, STEPS) as i:
                    act_step(i)

            @block.vector
            def _(dve):
                dve_step(0)
                with dve.Fori(1, STEPS) as i:
                    dve_step(i)

            @block.tensor
            def _(pe):
                pe_step(0)
                with pe.Fori(1, STEPS) as i:
                    pe_step(i)


INPUTS = ("x", "ctx_1024", "mask_1x1xSxS2_ik1",
          "L0_attn_Wq", "L0_attn_bq", "L0_attn_Wk", "L0_attn_bk", "L0_attn_Wv", "L0_attn_bv", "L0_attn_Wo", "L0_attn_bo",
          "L0_xattn_wq_w", "L0_xattn_wq_b", "L0_xattn_wk_w", "L0_xattn_wk_b", "L0_xattn_wv_w", "L0_xattn_wv_b",
          "L0_xattn_wo_w", "L0_xattn_wo_b", "L0_ffn_W_fc", "L0_ffn_ln_w", "L0_ffn_ln_b", "L0_ffn_W_proj")


def kernel(**inputs):
    import numpy as np
    import concourse.bacc as bacc
    from concourse.bass_utils import run_bass_kernel_spmd

    nc = bacc.Bacc("TRN2", target_bir_lowering=False, num_devices=1)
    arrays, aps = {}, []
    for name in INPUTS:
        a = np.ascontiguousarray(inputs[name])
        arrays["in_" + name] = a
        aps.append(nc.dram_tensor("in_" + name, a.shape, mybir.dt.from_np(a.dtype), kind="ExternalInput").ap())
    out = nc.dram_tensor("out_0", (B, S, D), F32, kind="ExternalOutput").ap()
    decoder_layer_kernel(nc, Inputs(*aps), out)
    result = run_bass_kernel_spmd(nc, [arrays], core_ids=[0])
    return result.results[0]["out_0"]
```

```python
from contextlib import ExitStack

import concourse.bass as bass
from concourse import mybir

F32, F16, BF16, I32 = mybir.dt.float32, mybir.dt.float16, mybir.dt.bfloat16, mybir.dt.int32
ALU = mybir.AluOpType
ACT = mybir.ActivationFunctionType
AX = mybir.AxisListType

P = 128
B, S, D = 128, 128, 256
H = 16
HD = D // H
F = 1024
G = 4
NG = B // G
T = G * S
KT = D // P
FT = F // P
PAIRS = H // 2
HALF = 64
STACK = 3 * HD
QUADS = H // 4
VW = 32
WS = 8.0
SHIFT = WS * WS
EXP_SCALE = 1.0 / (HD ** 0.5 * SHIFT)
LN_EPS = 1e-5
GAMMA_EPS = 1e-6
MASKED = 1e-9
NEG = -1e30
HI, LO = 0, 1
SPLITS = ((HI, HI), (LO, HI), (HI, LO))

SQ, SK, SV, SO, XQ, XK, XV, XO = range(8)
STACK_DMAS = 3 * FT


class Inputs:

    def __init__(self, x, ctx, mask, sWq, sbq, sWk, sbk, sWv, sbv, sWo, sbo,
                 xWq, xbq, xWk, xbk, xWv, xbv, xWo, xbo, Wfc, lnw, lnb, Wp):
        self.x, self.ctx, self.mask = x, ctx, mask
        self.weights = [sWq, sWk, sWv, sWo, xWq, xWk, xWv, xWo]
        self.qk_biases = [sbq, sbk, xbq, xbk]
        self.v_biases, self.o_biases = [sbv, xbv], [sbo, xbo]
        self.Wfc, self.lnw, self.lnb, self.Wp = Wfc, lnw, lnb, Wp


class Shared:

    def __init__(self, sb):
        self.WT = sb("WT", [P, 8, 2, KT, D], F16)
        self.wfcT = sb("wfcT", [P, KT, F], F16)
        self.wpT = sb("wpT", [P, FT, D], F16)
        self.bcol = sb("bcol", [P, 4, KT])
        self.boB = sb("boB", [P, 2, D])
        self.lnwB = sb("lnwB", [P, F])
        self.c2B = sb("c2B", [P, D])
        self.ident = sb("ident", [P, P])
        self.ident16 = sb("ident16", [P, P], F16)
        self.identb = sb("identb", [P, P], BF16)
        self.mhalf = sb("mhalf", [P, G])
        self.eps = sb("eps", [P, G])
        self.maskB4 = sb("maskB4", [P, 4, S], BF16)
        self.maskBT4 = sb("maskBT4", [P, G, S], BF16)
        self.maskcT = sb("maskcT", [P, S])
        self.cntW = sb("cntW", [P, 1])
        self.mfloor = sb("mfloor", [P, 1])


def allocators(nc, stack, program):
    sb = lambda name, shape, dt=F32: stack.enter_context(nc.sbuf_tensor(name, shape, dt))
    ps = lambda name, shape, dt=F32: stack.enter_context(nc.psum_tensor(name, shape, dt))
    sem = lambda name: program.enter_context(nc.semaphore(name))
    return sb, ps, sem


def wait(engine, sem, count):
    if not isinstance(count, int) or count > 0:
        engine.wait_ge(sem, count)


def decoder_layer_kernel(nc, ins, out):
    x2_dram = nc.dram_tensor("x2_scratch", (B, S, D), F32, kind="Internal").ap()
    with ExitStack() as stack:
        sb, _, _ = allocators(nc, stack, stack)
        sh = Shared(sb)
        setup(nc, stack, ins, sh)
        attention(nc, stack, ins, sh, x2_dram)
        ffn(nc, stack, sh, x2_dram, out)


def setup(nc, program, ins, sh):
    WT, wfcT, wpT, bcol, boB, lnwB, c2B = sh.WT, sh.wfcT, sh.wpT, sh.bcol, sh.boB, sh.lnwB, sh.c2B
    ident, ident16, identb, mhalf = sh.ident, sh.ident16, sh.identb, sh.mhalf
    maskB4, maskBT4, maskcT, cntW, mfloor = sh.maskB4, sh.maskBT4, sh.maskcT, sh.cntW, sh.mfloor

    with ExitStack() as stack:
        sb, ps, sem = allocators(nc, stack, program)
        wnat = sb("wnat", [P, 8, KT, D])
        fnat = sb("fnat", [P, 2, F * KT])
        neg = sb("neg", [P, 2, F * KT])
        junk = sb("junk", [P, F * KT])
        wpT32 = sb("wpT32", [P, FT, D])
        lnb_col = sb("lnb_col", [P, FT])
        bv_col = sb("bv_col", [P, 2 * KT])
        bvB = sb("bvB", [P, 2, 2 * KT, P], F16)
        lnbB = sb("lnbB", [P, FT, P])
        ones = sb("ones", [P, P])
        asum = sb("asum", [P, 2])
        thr = sb("thr", [P, 2])
        nthr = sb("nthr", [P, 2])
        imask = sb("imask", [P, S], I32)
        maskc = sb("maskc", [P, S])
        bank = ps("setup_bank", [P, 8, 512])

        w_in = sem("w_in")
        f_in, small_in, mask_in = sem("f_in"), sem("small_in"), sem("mask_in")
        zeroed, consts = sem("zeroed"), sem("consts")
        w_T, w_hi, w_lo = sem("w_T"), sem("w_hi"), sem("w_lo")
        abs_done, total_done, gamma_done, thr_done = sem("abs_done"), sem("total_done"), sem("gamma_done"), sem("thr_done")
        neg_done, tern_done, f_T, f_out = sem("neg_done"), sem("tern_done"), sem("f_T"), sem("f_out")
        lnb_done, c2_mm, c2_done = sem("lnb_done"), sem("c2_mm"), sem("c2_done")
        m_done, mc_done, m_T, m_out, cnt_done = sem("m_done"), sem("mc_done"), sem("m_T"), sem("m_out"), sem("cnt_done")
        scaled, bv_split, bo_mm, bo_done = sem("scaled"), sem("bv_split"), sem("bo_mm"), sem("bo_done")
        NSMALL = 4 + 2 + 2 + 1 + 1

        with nc.Block() as block:
            @block.sync
            def _(sp):
                for n, w in enumerate(ins.weights):
                    sp.dma_start(wnat[:, n], w.rearrange("(m p) i -> p m i", p=P)).then_inc(w_in, 16)
                for n, b in enumerate(ins.qk_biases):
                    sp.dma_start(bcol[:, n], b.rearrange("(m p) -> p m", p=P), allow_slow_non_contiguous=True).then_inc(small_in, 16)
                for n, b in enumerate(ins.v_biases):
                    sp.dma_start(bv_col[:, n * KT:(n + 1) * KT], b.rearrange("(m p) -> p m", p=P), allow_slow_non_contiguous=True).then_inc(small_in, 16)
                sp.dma_start(lnb_col[:, :], ins.lnb.rearrange("(t p) -> p t", p=P), allow_slow_non_contiguous=True).then_inc(small_in, 16)

            @block.scalar
            def _(act):
                act.dma_start(fnat[:, 0], ins.Wfc.rearrange("(t p) d -> p t d", p=P)).then_inc(f_in, 16)
                act.dma_start(fnat[:, 1], ins.Wp.rearrange("(t p) h -> p t h", p=P)).then_inc(f_in, 16)
                act.dma_start(imask[:, :], ins.mask[0, 0]).then_inc(mask_in, 16)
                for n in range(2):
                    act.dma_start(boB[:, n], ins.o_biases[n].partition_broadcast(P)).then_inc(small_in, 16)
                act.dma_start(lnwB[:, :], ins.lnw.partition_broadcast(P)).then_inc(small_in, 16)
                act.wait_ge(f_in, 32)
                for n in range(2):
                    if n:
                        act.wait_ge(abs_done, n)
                    nc.scalar.activation(junk[:, :], fnat[:, n], ACT.Abs, accum_out=asum[:, n:n + 1]).then_inc(abs_done, 1)
                for n in range(8):
                    act.wait_ge(w_T, n + 1)
                    nc.scalar.activation(WT[:, n, HI], bank[:, n, :].rearrange("p (k o) -> p k o", k=KT),
                                         ACT.Copy, scale=WS).then_inc(w_hi, 1)

            @block.gpsimd
            def _(pool):
                for t in (ident, ident16, identb):
                    nc.gpsimd.memset(t[:, :], 0.0).then_inc(zeroed, 1)
                nc.gpsimd.memset(ones[:, :], 1.0).then_inc(zeroed, 1)
                nc.gpsimd.memset(mhalf[:, :], -0.5).then_inc(zeroed, 1)
                nc.gpsimd.memset(sh.eps[:, :], LN_EPS).then_inc(zeroed, 1)
                pool.wait_ge(zeroed, 6)
                for t in (ident, ident16, identb):
                    nc.gpsimd.affine_select(out=t[:, :], in_=t[:, :], compare_op=ALU.not_equal, fill=1.0,
                                            base=0, pattern=[[-1, P]], channel_multiplier=1).then_inc(consts, 1)

            @block.vector
            def _(dve):
                dve.wait_ge(total_done, 1)
                nc.vector.tensor_scalar(thr[:, :], bank[:, 7, 0:2], 1.0 / (F * D), GAMMA_EPS, ALU.mult, ALU.add).then_inc(gamma_done, 1)
                dve.wait_ge(gamma_done, 1)
                nc.vector.tensor_scalar(nthr[:, :], thr[:, :], -0.5, None, ALU.mult).then_inc(thr_done, 1)
                dve.wait_ge(thr_done, 1)
                nc.vector.tensor_scalar(thr[:, :], thr[:, :], 0.5, None, ALU.mult).then_inc(thr_done, 1)
                dve.wait_ge(thr_done, 2)
                for n in range(2):
                    nc.vector.tensor_scalar(neg[:, n], fnat[:, n], nthr[:, n:n + 1], None, ALU.is_lt).then_inc(neg_done, 1)
                for n in range(2):
                    dve.wait_ge(neg_done, n + 1)
                    nc.vector.scalar_tensor_tensor(fnat[:, n], fnat[:, n], thr[:, n:n + 1], neg[:, n],
                                                   ALU.is_gt, ALU.subtract).then_inc(tern_done, 1)
                for n in range(8):
                    dve.wait_ge(w_hi, n + 1)
                    nc.vector.scalar_tensor_tensor(WT[:, n, LO].rearrange("p k o -> p (k o)"), bank[:, n, :], WS,
                                                   WT[:, n, HI].rearrange("p k o -> p (k o)"),
                                                   ALU.mult, ALU.subtract).then_inc(w_lo, 1)
                dve.wait_ge(small_in, 16 * NSMALL)
                nc.vector.tensor_scalar(bcol[:, :, :], bcol[:, :, :], WS, None, ALU.mult).then_inc(scaled, 1)
                for c in range(2 * KT):
                    last = nc.vector.tensor_copy(bvB[:, HI, c], bv_col[:, c:c + 1].broadcast_to([P, P]))
                last.then_inc(bv_split, 1)
                dve.wait_ge(bv_split, 1)
                for c in range(2 * KT):
                    last = nc.vector.tensor_tensor(bvB[:, LO, c], bv_col[:, c:c + 1].broadcast_to([P, P]), bvB[:, HI, c], ALU.subtract)
                last.then_inc(bv_split, 1)
                for t in range(FT):
                    last = nc.vector.tensor_copy(lnbB[:, t], lnb_col[:, t:t + 1].broadcast_to([P, P]))
                last.then_inc(lnb_done, 1)
                for kt in range(KT):
                    dve.wait_ge(f_T, kt + 1)
                    nc.vector.tensor_copy(wfcT[:, kt].rearrange("p (a h) -> p a h", a=2), bank[:, 2 * kt:2 * kt + 2, :]).then_inc(f_out, 1)
                dve.wait_ge(f_T, KT + 1)
                nc.vector.tensor_copy(wpT[:, :, :].rearrange("p (a t) d -> p a (t d)", a=4), bank[:, 4:8, :]).then_inc(f_out, 1)
                nc.vector.tensor_copy(wpT32[:, :, :].rearrange("p (a t) d -> p a (t d)", a=4), bank[:, 4:8, :]).then_inc(f_out, 1)
                dve.wait_ge(c2_mm, 1)
                nc.vector.tensor_copy(c2B[:, :], bank[:, 0, 0:D]).then_inc(c2_done, 1)
                dve.wait_ge(bo_mm, 1)
                nc.vector.scalar_tensor_tensor(boB[:, :, :].rearrange("p n d -> p (n d)"), bank[:, 2, :], 1.0 / WS,
                                               boB[:, :, :].rearrange("p n d -> p (n d)"), ALU.mult, ALU.add).then_inc(bo_done, 1)
                dve.wait_ge(mask_in, 16)
                nc.vector.tensor_copy(maskc[:, :], imask[:, :]).then_inc(m_done, 1)
                dve.wait_ge(m_done, 1)
                nc.vector.tensor_scalar(maskc[:, :], maskc[:, :], 0.0, None, ALU.is_equal).then_inc(mc_done, 1)
                dve.wait_ge(mc_done, 1)
                nc.vector.tensor_reduce(cntW[:, :], maskc[:, :], AX.X, ALU.add).then_inc(cnt_done, 1)
                for n in range(4):
                    nc.vector.tensor_scalar(maskB4[:, n], maskc[:, :], NEG, None, ALU.mult)
                dve.wait_ge(cnt_done, 1)
                nc.vector.tensor_scalar(mfloor[:, :], cntW[:, :], 0.0, NEG, ALU.is_le, ALU.mult).then_inc(cnt_done, 1)
                dve.wait_ge(cnt_done, 2)
                nc.vector.tensor_scalar(mfloor[:, :], mfloor[:, :], MASKED * HD ** 0.5 * SHIFT, None, ALU.add).then_inc(cnt_done, 1)
                nc.vector.tensor_scalar(cntW[:, :], cntW[:, :], WS, None, ALU.mult).then_inc(cnt_done, 1)
                dve.wait_ge(m_T, 1)
                nc.vector.tensor_copy(maskcT[:, :], bank[:, 1, 0:S]).then_inc(m_out, 1)
                for n in range(G):
                    nc.vector.tensor_scalar(maskBT4[:, n], bank[:, 1, 0:S], NEG, None, ALU.mult).then_inc(m_out, 1)

            @block.tensor
            def _(pe):
                pe.wait_ge(consts, 3)
                pe.wait_ge(abs_done, 2)
                nc.tensor.matmul(bank[:, 7, 0:2], ones[:, :], asum[:, :], start=True, stop=True).then_inc(total_done, 1)
                pe.wait_ge(gamma_done, 1)
                pe.wait_ge(w_in, 16 * 8)
                for n in range(8):
                    for mt in range(KT):
                        for kt in range(KT):
                            last = nc.tensor.transpose(bank[:, n, kt * D + mt * P:kt * D + (mt + 1) * P],
                                                       wnat[:, n, mt, kt * P:(kt + 1) * P], ident[:, :])
                    last.then_inc(w_T, 1)
                pe.wait_ge(w_lo, 8)
                pe.wait_ge(tern_done, 2)
                fc = fnat[:, 0].rearrange("p (t d) -> p t d", t=FT)
                pj = fnat[:, 1].rearrange("p (t h) -> p t h", t=KT)
                for kt in range(KT):
                    for t in range(FT):
                        last = nc.tensor.transpose(bank[:, 2 * kt + t // 4, (t % 4) * P:(t % 4 + 1) * P],
                                                   fc[:, t, kt * P:(kt + 1) * P], ident[:, :])
                    last.then_inc(f_T, 1)
                for t in range(FT):
                    for m in range(KT):
                        o = (t % 2) * D + m * P
                        last = nc.tensor.transpose(bank[:, 4 + t // 2, o:o + P], pj[:, m, t * P:(t + 1) * P], ident[:, :])
                last.then_inc(f_T, 1)
                pe.wait_ge(f_out, 4)
                pe.wait_ge(lnb_done, 1)
                for t in range(FT):
                    last = nc.tensor.matmul(bank[:, 0, 0:D], lnbB[:, t], wpT32[:, t], start=(t == 0), stop=(t == FT - 1))
                last.then_inc(c2_mm, 1)
                pe.wait_ge(bv_split, 2)
                for n, wo in enumerate((SO, XO)):
                    for m, (a, wp) in enumerate(SPLITS):
                        for kt in range(KT):
                            last = nc.tensor.matmul(bank[:, 2, n * D:(n + 1) * D], bvB[:, a, n * KT + kt], WT[:, wo, wp, kt],
                                                    start=(m == 0 and kt == 0), stop=(m == 2 and kt == KT - 1))
                last.then_inc(bo_mm, 1)
                pe.wait_ge(mc_done, 1)
                nc.tensor.transpose(bank[:, 1, 0:S], maskc[:, :], ident[:, :]).then_inc(m_T, 1)


class Chain:

    def __init__(self, name, sb, ps, sem, first_weight, prob):
        n = name
        self.cross = name == "cross"
        self.wq, self.wk, self.wv, self.wo = range(first_weight, first_weight + 4)
        self.which = 1 if self.cross else 0
        self.pb = 2 if self.cross else 0
        self.tb = 0 if self.cross else 2
        self.src = sb(n + "_src", [P, G, D])
        self.stats = sb(n + "_stats", [P, G, 6])
        self.mv = sb(n + "_mv", [P, G, 2])
        self.ve = sb(n + "_ve", [P, G])
        self.rstd = sb(n + "_rstd", [P, G])
        self.xn = sb(n + "_xn", [P, G, D])
        self.xb = sb(n + "_xb", [P, G, D])
        self.xs = sb(n + "_xs", [P, 2, G, D], F16)
        self.xhl = sb(n + "_xhl", [P, 2, KT, T], F16)
        self.qk = sb(n + "_qk", [P, 4, KT, T], F16)
        self.stk = sb(n + "_stk", [P, 2, FT // 2, KT, T], F16)
        self.vals = sb(n + "_vals", [P, G, H, VW])
        self.prob = prob
        self.oT = self.qk[:, :, :, :].rearrange("p a k t -> p (a k t)").bitcast(F32).rearrange("p (q t) -> p q t", q=QUADS)
        self.mx = sb(n + "_mx", [P, G * H])
        self.negm = sb(n + "_negm", [P, G * H], F16)
        self.negmT = sb(n + "_negmT", [H, T], F16)
        self.rec = sb(n + "_rec", [P, QUADS, G * 4])
        self.att = sb(n + "_att", [P, G, D])
        self.asp = sb(n + "_asp", [P, 2, G, D], F16)
        self.ahl = sb(n + "_ahl", [P, 2, KT, T], F16)
        self.bk = ps(n + "_bk", [P, 4, 512])
        if not self.cross:
            self.loaded = sem("self_loaded")
        self.stats_done = sem(n + "_stats_done")
        self.moments = sem(n + "_moments")
        self.var_ready = sem(n + "_var_ready")
        self.rstd_ready = sem(n + "_rstd_ready")
        self.xn_ready = sem(n + "_xn_ready")
        self.xb_ready = sem(n + "_xb_ready")
        self.xs_hi = sem(n + "_xs_hi")
        self.xs_lo = sem(n + "_xs_lo")
        self.xT_ready = sem(n + "_xT_ready")
        self.xhl_ready = sem(n + "_xhl_ready")
        self.qk_mm = sem(n + "_qk_mm")
        self.qk_hi = sem(n + "_qk_hi")
        self.qk_lo = sem(n + "_qk_lo")
        self.v_mm = sem(n + "_v_mm")
        self.v_ready = sem(n + "_v_ready")
        self.stacked = sem(n + "_stacked")
        self.s_mm = sem(n + "_s_mm")
        self.max_done = sem(n + "_max_done")
        self.negm_ready = sem(n + "_negm_ready")
        self.mT_ready = sem(n + "_mT_ready")
        self.mT_out = sem(n + "_mT_out")
        self.m_in = sem(n + "_m_in")
        self.st_mm = sem(n + "_st_mm")
        self.exp_done = sem(n + "_exp_done")
        self.pv_done = sem(n + "_pv_done")
        self.o_out = sem(n + "_o_out")
        self.oT_ready = sem(n + "_oT_ready")
        if self.cross:
            self.den_ready = sem("cross_den_ready")
        self.rec_ready = sem(n + "_rec_ready")
        self.ao_ready = sem(n + "_ao_ready")
        self.as_hi = sem(n + "_as_hi")
        self.as_lo = sem(n + "_as_lo")
        self.aT_ready = sem(n + "_aT_ready")
        self.ahl_ready = sem(n + "_ahl_ready")
        self.op_mm = sem(n + "_op_mm")
        self.op_out = sem(n + "_op_out")
        self.y_ready = sem(n + "_y_ready")


def attention(nc, program, ins, sh, x2_dram):
    x_groups = ins.x.rearrange("(n b) s d -> n s b d", b=G)
    ctx_groups = ins.ctx.rearrange("(n b) s d -> n s b d", b=G)
    x2_groups = x2_dram.rearrange("(n b) s d -> n s b d", b=G)
    with ExitStack() as stack:
        sb, ps, sem = allocators(nc, stack, program)
        prob = sb("prob", [P, 2, 4, T])
        slf = Chain("self", sb, ps, sem, 0, prob)
        crs = Chain("cross", sb, ps, sem, 4, prob)
        cin = sb("ctx_in", [P, G, D])
        cs = sb("ctx_s", [P, 2, G, D], F16)
        chl = sb("ctx_hl", [P, 2, KT, T], F16)
        earg = sb("earg", [P, G * H])
        ew = sb("ew", [P, G, H])
        ue = sb("ue", [P, G, H, HD + 1])
        total = sb("total", [P, QUADS, G, 4, HD + 1])
        held = sb("held_wait", [P, 1])
        primed = sem("primed")
        c_loaded, cs_hi, cs_lo = sem("c_loaded"), sem("cs_hi"), sem("cs_lo")
        cT_ready, chl_ready = sem("cT_ready"), sem("chl_ready")
        earg_ready, ew_ready, ecnt_ready = sem("earg_ready"), sem("ew_ready"), sem("ecnt_ready")
        u_mm, ue_ready, stored = sem("u_mm"), sem("ue_ready"), sem("stored")

        def present(g):
            return g if not isinstance(g, int) or 0 <= g < NG else None

        def step(slot, i):
            slot(crs, slf, present(i - 1), present(i), present(i + 1), present(i))
            slot(slf, crs, present(i + 1), present(i - 1), present(i), present(i + 2))

        def steps(engine, slot):
            for i in range(-2, 2):
                step(slot, i)
            with engine.Fori(2, NG - 2) as i:
                step(slot, i)
            for i in range(NG - 2, NG + 1):
                step(slot, i)


        def out_bank(ch, qd):
            return ch.bk[:, 2, :] if qd == QUADS - 1 else (slf if ch.cross else crs).bk[:, 2 + qd % 2, :]

        def turned_bank(ch, qd):
            return ch.bk[:, 1, :] if qd == QUADS - 1 else (slf if ch.cross else crs).bk[:, (0, 1, 3)[qd], :]


        def stack_rows(sp, ch, g, block, heads):
            parts, done, count = ((slice(1, 3), ch.qk_hi, 4), (slice(0, 3, 2), ch.qk_lo, 2), (slice(1, 4, 2), ch.qk_lo, 4))[block]
            if not heads:
                return
            sp.wait_ge(done, 4 * g + count)
            for j in heads:
                rows, to = slice(HD * j, HD * j + HD), HALF * (j % 2) + HD * block
                sp.dma_start(ch.stk[to:to + HD, :, j // 2], ch.qk[rows, parts]).then_inc(ch.stacked, 16)

        EARLY = {slf: 3, crs: 4}

        def sp_slot(sp, y, x, att, tail, proj, norm):
            if x.cross and proj is not None and present(proj + 1) is not None:
                ctx_group = ctx_groups[proj + 1]
                sp.wait_ge(cs_lo, proj + 1)
                sp.dma_start(cin[:, :, :], ctx_group).then_inc(c_loaded, 16)
            early = EARLY[x]
            if proj is not None:
                stack_rows(sp, x, proj, 0, range(early))
            if att is not None:
                sp.wait_ge(y.mT_out, att + 1)
                for r in range(2):
                    sp.dma_start(y.stk[HALF * r + STACK:HALF * (r + 1), 0].rearrange("p a k t -> p (a k) t"),
                                 y.negmT[:, :].unsqueeze(1).broadcast_to([H, PAIRS, T])).then_inc(y.m_in, 16)
            if proj is not None:
                stack_rows(sp, x, proj, 0, range(early, FT))
                stack_rows(sp, x, proj, 1, range(FT))
                stack_rows(sp, x, proj, 2, range(FT))
                if not x.cross and present(proj + 1) is not None:
                    x_group = x_groups[proj + 1]
                    sp.wait_ge(slf.xb_ready, proj + 1)
                    sp.dma_start(slf.src[:, :, :], x_group).then_inc(slf.loaded, 16)
            if x.cross and tail is not None:
                x2_group = x2_groups[tail]
                sp.wait_ge(crs.y_ready, tail + 1)
                sp.dma_start(x2_group, crs.att[:, :, :]).then_inc(stored, 16)


        FIRST, LAST = slice(0, D - 4 * HD), slice(D - 4 * HD, D)

        def pool_slot(pool, y, x, att, tail, proj, norm):
            def deviations():
                if norm is not None:
                    pool.wait_ge(y.var_ready, norm + 1)
                    wait(pool, y.xn_ready, norm)
                    nc.gpsimd.tensor_tensor(y.rstd[:, :], y.ve[:, :], sh.mhalf[:, :], ALU.pow).then_inc(y.rstd_ready, 1)

            def lo(src, split, hi_ready, lo_ready, count, cols=slice(0, D)):
                pool.wait_ge(hi_ready, count)
                nc.gpsimd.tensor_tensor(split[:, LO, :, cols], src[:, :, cols], split[:, HI, :, cols],
                                        ALU.subtract).then_inc(lo_ready, 1)

            if tail is not None:
                lo(x.att, x.asp, x.as_hi, x.as_lo, 2 * tail + 2, LAST)
            if x.cross:
                deviations()
                if norm is not None:
                    lo(y.xn, y.xs, y.xs_hi, y.xs_lo, norm + 1)
            if tail is not None:
                pool.wait_ge(x.xb_ready, tail + 1)
                if not x.cross:
                    wait(pool, crs.xb_ready, tail)
                pool.wait_ge(x.op_out, tail + 1)
                y_out = crs.att if x.cross else crs.src
                nc.gpsimd.tensor_tensor(y_out[:, :, :], x.att[:, :, :], x.xb[:, :, :], ALU.add).then_inc(x.y_ready, 1)
            if proj is not None:
                pool.wait_ge(x.xn_ready, proj + 1)
                wait(pool, x.y_ready, proj)
                nc.gpsimd.tensor_tensor(x.xb[:, :, :], x.src[:, :, :], sh.boB[:, x.which:x.which + 1, :].broadcast_to([P, G, D]),
                                        ALU.add).then_inc(x.xb_ready, 1)
            if not x.cross:
                deviations()
                if norm is not None:
                    lo(cin, cs, cs_hi, cs_lo, norm + 1)
                    lo(y.xn, y.xs, y.xs_hi, y.xs_lo, norm + 1)
            if att is not None:
                lo(y.att, y.asp, y.as_hi, y.as_lo, 2 * att + 1, FIRST)


        def qk_bank(ch, n):
            return ch.bk[:, ch.pb + n % 2, :]

        def act_qk(act, ch, g, n):
            act.wait_ge(ch.qk_mm, 4 * g + n + 1)
            if n == 0:
                wait(act, ch.stacked, 16 * STACK_DMAS * g)
            act.activation(ch.qk[:, 1 + n // 2, n % 2], qk_bank(ch, n), ACT.Identity,
                           bias=sh.bcol[:, 2 * ch.which + n // 2, n % 2:n % 2 + 1]).then_inc(ch.qk_hi, 1)

        def act_slot(y, x, att, tail, proj, norm):
            act = nc.scalar

            def both(turned, hl, bank, ready, g):
                if g is not None:
                    act.wait_ge(turned, g + 1)
                    act.activation(hl[:, :].rearrange("p a k t -> p a (k t)"), x.bk[:, bank:bank + 2, :].bitcast(F16),
                                   ACT.Copy).then_inc(ready, 1)

            def split_context():
                if norm is not None:
                    act.wait_ge(c_loaded, 16 * norm + 16)
                    act.activation(cs[:, HI], cin[:, :, :], ACT.Copy).then_inc(cs_hi, 1)

            def split_norm():
                if norm is not None:
                    act.wait_ge(y.xn_ready, norm + 1)
                    act.activation(y.xs[:, HI], y.xn[:, :, :], ACT.Copy).then_inc(y.xs_hi, 1)

            def split_outputs(ch, g, quads, cols):
                if g is not None:
                    act.wait_ge(ch.ao_ready, 4 * g + quads)
                    act.activation(ch.asp[:, HI, :, cols], ch.att[:, :, cols], ACT.Copy).then_inc(ch.as_hi, 1)

            def tiles(*some):
                if proj is not None:
                    for n in some:
                        act_qk(act, x, proj, n)

            def values_out():
                if proj is not None:
                    for n in range(2):
                        act.wait_ge(x.v_mm, 2 * proj + n + 1)
                        act.activation(x.vals[:, 2 * n:2 * n + 2, :, 0:HD].rearrange("p b h d -> p (b h) d"),
                                       x.bk[:, x.pb + n, :].rearrange("p (a d) -> p a d", d=HD), ACT.Copy).then_inc(x.v_ready, 1)

            def products_out():
                if tail is not None:
                    act.wait_ge(x.op_mm, tail + 1)
                    act.activation(x.att[:, :, :].rearrange("p b d -> p (b d)"), x.bk[:, x.tb:x.tb + 2, :].rearrange("p a d -> p (a d)"),
                                   ACT.Copy, scale=1.0 / WS).then_inc(x.op_out, 1)

            if x.cross:
                both(x.xT_ready, x.xhl, x.pb, x.xhl_ready, proj)
                split_outputs(x, tail, 4, LAST)
                both(cT_ready, chl, x.tb, chl_ready, proj)
                tiles(0, 1)
                both(x.aT_ready, x.ahl, x.tb, x.ahl_ready, tail)
                tiles(2, 3)
            else:
                split_outputs(x, tail, 4, LAST)
                both(x.xT_ready, x.xhl, x.pb, x.xhl_ready, proj)
                both(x.aT_ready, x.ahl, x.tb, x.ahl_ready, tail)
                tiles(0, 1, 2, 3)
            if att is not None:
                if y.cross:
                    act.wait_ge(earg_ready, att + 1)
                    act.activation(ew[:, :, :].rearrange("p b h -> p (b h)"), earg[:, :], ACT.Exp, scale=HD ** -0.5).then_inc(ew_ready, 1)
                act.wait_ge(y.mT_ready, att + 1)
                wait(act, y.m_in, 32 * att)
                act.activation(y.negmT[:, :], y.bk[0:H, 0, 0:T // 2].bitcast(F16), ACT.Copy).then_inc(y.mT_out, 1)

            if x.cross:
                values_out()
                if att is None:
                    products_out()
            else:
                products_out()
                values_out()
            if att is not None:
                for n in range(H):
                    qd = n // 4
                    if n == 4 and x.cross:
                        products_out()
                    if n == 8 and y.cross:
                        split_context()
                    if n == (12 if y.cross else 8):
                        split_norm()
                    if n % 4 == 0 and qd > 1:
                        act.wait_ge(y.pv_done, 4 * att + qd - 1)
                    act.wait_ge(y.st_mm, 16 * att + n + 1)
                    act.activation(y.prob[:, qd % 2, n % 4], y.bk[:, n % 4, :], ACT.Exp, scale=EXP_SCALE).then_inc(y.exp_done, 1)
                act.wait_ge(y.pv_done, 4 * att + QUADS)
                act.wait_ge(y.o_out, 4 * att + QUADS - 1)
                act.activation(y.oT[:, QUADS - 1], out_bank(y, QUADS - 1), ACT.Copy).then_inc(y.o_out, 1)
            else:
                if y.cross:
                    split_context()
                split_norm()
            split_outputs(y, att, 3, FIRST)


        def dve_qk(dve, ch, g, n):
            dve.wait_ge(ch.qk_hi, 4 * g + n + 1)
            dve.scalar_tensor_tensor(ch.qk[:, 3 * (n // 2), n % 2], qk_bank(ch, n),
                                     sh.bcol[:, 2 * ch.which + n // 2, n % 2:n % 2 + 1],
                                     ch.qk[:, 1 + n // 2, n % 2], ALU.add, ALU.subtract).then_inc(ch.qk_lo, 1)

        def dve_max(dve, ch, g, m):
            dve.wait_ge(ch.s_mm, 8 * g + m + 1)
            o = 2 * (m % 2)
            dve.tensor_reduce(ch.mx[:, 8 * m:8 * m + 8].rearrange("p (j r) -> p r j", r=2),
                              ch.bk[:, o:o + 2, :].rearrange("p r (j k) -> p r j k", j=4), AX.X, ALU.max).then_inc(ch.max_done, 1)

        def dve_normalise(dve, ch, g, qd):
            dve.wait_ge(ch.oT_ready, 4 * g + qd + 1)
            o = turned_bank(ch, qd).rearrange("p (b h c) -> p b h c", b=G, h=4)[:, :, :, 0:HD + 1]
            if qd == 0:
                if ch.cross:
                    wait(dve, stored, 16 * g)
                else:
                    wait(dve, ch.y_ready, g)
            if ch.cross:
                if qd == 0:
                    dve.wait_ge(ue_ready, 2 * g + 2)
                    dve.wait_ge(ecnt_ready, g + 1)
                dve.tensor_tensor(total[:, qd], o, ue[:, :, 4 * qd:4 * qd + 4, :], ALU.add).then_inc(ch.den_ready, 1)
                dve.wait_ge(ch.den_ready, 4 * g + qd + 1)
                o = total[:, qd]
            num, den = o[:, :, :, 0:HD], o[:, :, :, HD]
            dve.reciprocal(ch.rec[:, qd].rearrange("p (b h) -> p b h", b=G), den).then_inc(ch.rec_ready, 1)
            dve.wait_ge(ch.rec_ready, 4 * g + qd + 1)
            dve.tensor_tensor(ch.att[:, :, qd * 4 * HD:(qd + 1) * 4 * HD].rearrange("p b (h d) -> p b h d", d=HD), num,
                              ch.rec[:, qd].rearrange("p (b h) -> p b h", b=G).unsqueeze(3).broadcast_to([P, G, 4, HD]),
                              ALU.mult).then_inc(ch.ao_ready, 1)

        def dve_slot(y, x, att, tail, proj, norm):
            dve = nc.vector

            def maxima(*eights):
                if att is not None:
                    for m in eights:
                        dve_max(dve, y, att, m)

            def tiles(*some):
                if proj is not None:
                    for n in some:
                        dve_qk(dve, x, proj, n)

            maxima(0)
            if tail is not None:
                dve_normalise(dve, x, tail, QUADS - 1)
            maxima(1, 2, 3)
            if x.cross:
                tiles(0)
                maxima(4)
                tiles(1)
                maxima(5, 6, 7)
            else:
                maxima(4)
                tiles(0)
                maxima(5)
                tiles(1)
                maxima(6, 7)
            if att is not None:
                dve.wait_ge(y.max_done, 8 * att + 8)
                if y.cross:
                    dve.tensor_scalar(y.negm[:, :], y.mx[:, :], sh.mfloor[:, :], -1.0 / SHIFT, ALU.max, ALU.mult).then_inc(y.negm_ready, 1)
                    dve.wait_ge(y.negm_ready, att + 1)
                    dve.tensor_scalar(earg[:, :], y.negm[:, :], 0.0, MASKED * HD ** 0.5, ALU.min, ALU.add).then_inc(earg_ready, 1)
                else:
                    dve.tensor_scalar(y.negm[:, :], y.mx[:, :], -1.0 / SHIFT, None, ALU.mult).then_inc(y.negm_ready, 1)
            tiles(2, 3)
            if att is not None and y.cross:
                dve.wait_ge(ew_ready, att + 1)
                dve.tensor_scalar(ue[:, :, :, HD], ew[:, :, :], sh.cntW[:, :], None, ALU.mult).then_inc(ecnt_ready, 1)
                for n in range(2):
                    dve.wait_ge(u_mm, 2 * att + n + 1)
                    dve.tensor_tensor(ue[:, 2 * n:2 * n + 2, :, 0:HD].rearrange("p b h d -> p (b h) d"),
                                      y.bk[:, 2 + n, :].rearrange("p (a d) -> p a d", d=HD),
                                      ew[:, 2 * n:2 * n + 2].rearrange("p b h -> p (b h)").unsqueeze(2).broadcast_to([P, 2 * H, HD]),
                                      ALU.mult).then_inc(ue_ready, 1)
            if norm is not None:
                if y.cross:
                    dve.wait_ge(slf.y_ready, norm + 1)
                else:
                    dve.wait_ge(slf.loaded, 16 * norm + 16)
                for b in range(G):
                    dve.bn_stats(y.stats[:, b], y.src[:, b]).then_inc(y.stats_done, 1)
                dve.wait_ge(y.stats_done, 4 * norm + 4)
                dve.memset(held[:, :], 0.0)
                for b in range(G):
                    last = dve.bn_aggr(y.mv[:, b], y.stats[:, b])
                last.then_inc(y.moments, 1)
                dve.wait_ge(y.moments, norm + 1)
                dve.tensor_scalar(y.ve[:, :], y.mv[:, :, 1], LN_EPS, None, ALU.add).then_inc(y.var_ready, 1)
            if norm is not None:
                dve.wait_ge(y.rstd_ready, norm + 1)
                for b in range(G):
                    last = dve.tensor_scalar(y.xn[:, b], y.src[:, b], y.mv[:, b, 0:1], y.rstd[:, b:b + 1],
                                             ALU.subtract, ALU.mult)
                last.then_inc(y.xn_ready, 1)
            if att is not None:
                for qd in range(QUADS - 1):
                    dve.wait_ge(y.pv_done, 4 * att + qd + 1)
                    dve.tensor_copy(y.oT[:, qd], out_bank(y, qd)).then_inc(y.o_out, 1)
                    if qd:
                        dve_normalise(dve, y, att, qd - 1)
                dve_normalise(dve, y, att, QUADS - 2)


        def tile_product(ch, bank, w, tile, moving):
            for n, (a, wp) in enumerate(SPLITS):
                for kt in range(KT):
                    last = nc.tensor.matmul(ch.bk[:, bank, :], sh.WT[:, w, wp, kt, tile * P:(tile + 1) * P], moving[:, a, kt, :],
                                            start=(n == 0 and kt == 0), stop=(n == 2 and kt == KT - 1))
            return last

        def token_product(ch, bank, w, b, tokens):
            for n, (a, wp) in enumerate(SPLITS):
                for kt in range(KT):
                    last = nc.tensor.matmul(ch.bk[:, bank, (b % 2) * D:(b % 2 + 1) * D], tokens[:, a, kt, b * S:(b + 1) * S],
                                            sh.WT[:, w, wp, kt, :], start=(n == 0 and kt == 0), stop=(n == 2 and kt == KT - 1))
            return last

        def turn_split(ch, bank, split):
            for part in (HI, LO):
                out = ch.bk[:, bank + part, :].bitcast(F16)
                for kt in range(KT):
                    for b in range(G):
                        at = kt * T + b * S
                        last = nc.tensor.transpose(out[:, at:at + S], split[:, part, b, kt * P:(kt + 1) * P], sh.ident16[:, :])
            return last

        def pe_scores(pe, ch, g, m):
            b, eight = divmod(m, 2)
            if m == 0:
                pe.wait_ge(ch.stacked, 16 * STACK_DMAS * (g + 1))
                pe.wait_ge(ch.v_ready, 2 * g + 2)
                wait(pe, ch.op_out, g)
            if m > 1:
                pe.wait_ge(ch.max_done, 8 * g + m - 1)
            if ch.cross:
                for r in range(2):
                    pe.matmul(ch.bk[:, 2 * (m % 2) + r, :], sh.identb[:, :], sh.maskB4[:, :, :], start=True, stop=False, skip_group_check=True)
            for j in range(4):
                for r in range(2):
                    rows = slice(HALF * r, HALF * r + STACK)
                    last = pe.matmul(ch.bk[:, 2 * (m % 2) + r, j * S:(j + 1) * S], ch.stk[rows, 0, j, eight, b * S:(b + 1) * S],
                                     ch.stk[rows, 1, j, eight, b * S:(b + 1) * S], start=not ch.cross, stop=True, skip_group_check=True)
            last.then_inc(ch.s_mm, 1)

        def pe_shifted(pe, ch, g, n):
            if n == 0:
                pe.wait_ge(ch.m_in, 32 * (g + 1))
            if n in (2, 3) and ch.cross:
                pe.wait_ge(ue_ready, 2 * g + n - 1)
            if n > 3:
                pe.wait_ge(ch.exp_done, 16 * g + n - 3)
            if ch.cross:
                pe.matmul(ch.bk[:, n % 4, :], sh.identb[:, :], sh.maskBT4[:, :, :], start=True, stop=False, skip_group_check=True)
            rows = slice(HALF * (n % 2), HALF * (n % 2 + 1))
            for b in range(G):
                last = pe.matmul(ch.bk[:, n % 4, b * S:(b + 1) * S], ch.stk[rows, 1, n // 2 % 4, n // 8, b * S:(b + 1) * S],
                                 ch.stk[rows, 0, n // 2 % 4, n // 8, b * S:(b + 1) * S], start=not ch.cross, stop=True, skip_group_check=True)
            last.then_inc(ch.st_mm, 1)

        def pe_values(pe, ch, g, qd):
            pe.wait_ge(ch.exp_done, 16 * g + 4 * qd + 4)
            if qd == 2:
                pe.wait_ge(ch.o_out, 4 * g + 1)
            for b in range(G):
                for jq in range(4):
                    last = pe.matmul(out_bank(ch, qd)[32 * jq:32 * jq + VW, b * S:(b + 1) * S], ch.vals[:, b, 4 * qd + jq, :],
                                     ch.prob[:, qd % 2, jq, b * S:(b + 1) * S], start=True, stop=True, skip_group_check=True)
            last.then_inc(ch.pv_done, 1)

        def pe_turn_outputs(pe, ch, g, qd):
            pe.wait_ge(ch.o_out, 4 * g + qd + 1)
            for b in range(G):
                last = pe.transpose(turned_bank(ch, qd)[:, b * S:(b + 1) * S], ch.oT[:, qd, b * S:(b + 1) * S], sh.ident[:, :])
            last.then_inc(ch.oT_ready, 1)

        def pe_slot(y, x, att, tail, proj, norm):
            pe = nc.tensor
            other = chl if x.cross else x.xhl

            def scores(*eights):
                if att is not None:
                    for m in eights:
                        if m == 1 and tail is not None:
                            pe.wait_ge(x.ao_ready, 4 * tail + 3)
                        pe_scores(pe, y, att, m)

            def tiles(*some):
                if proj is not None:
                    for n in some:
                        if n > 1:
                            pe.wait_ge(x.qk_lo, 4 * proj + n - 1)
                        tile_product(x, x.pb + n % 2, (x.wq, x.wk)[n // 2], n % 2, other if n > 1 else x.xhl).then_inc(x.qk_mm, 1)

            def values():
                if proj is not None:
                    for b in range(G):
                        if b % 2 == 0:
                            pe.wait_ge(x.qk_lo, 4 * proj + 3 + b // 2)
                        last = token_product(x, x.pb + b // 2, x.wv, b, other)
                        if b % 2:
                            last.then_inc(x.v_mm, 1)

            def products(*batches):
                if tail is not None:
                    if 0 in batches:
                        pe.wait_ge(x.ahl_ready, tail + 1)
                    for b in batches:
                        last = token_product(x, x.tb + b // 2, x.wo, b, x.ahl)
                        if b == G - 1:
                            last.then_inc(x.op_mm, 1)

            def turn_input():
                pe.wait_ge(x.xs_lo, proj + 1)
                turn_split(x, x.pb, x.xs).then_inc(x.xT_ready, 1)

            def turn_att():
                if tail is not None:
                    pe.wait_ge(x.as_lo, 2 * tail + 2)
                    turn_split(x, x.tb, x.asp).then_inc(x.aT_ready, 1)

            def turn_maxima():
                if att is not None:
                    pe.wait_ge(y.negm_ready, att + 1)
                    for b in range(G):
                        last = pe.transpose(y.bk[0:H, 0, b * S // 2:(b + 1) * S // 2].bitcast(F16), y.negm[:, b * H:(b + 1) * H], sh.ident16[:, :])
                    last.then_inc(y.mT_ready, 1)

            scores(0)
            if tail is not None:
                pe_turn_outputs(pe, x, tail, QUADS - 1)
            if x.cross:
                if proj is not None:
                    turn_input()
                scores(1)
                scores(2)
                if proj is not None:
                    pe.wait_ge(cs_lo, proj + 1)
                    if tail is not None:
                        pe.wait_ge(x.ao_ready, 4 * tail + 4)
                    turn_split(x, x.tb, cs).then_inc(cT_ready, 1)
                scores(3)
                if proj is not None:
                    pe.wait_ge(x.xhl_ready, proj + 1)
                tiles(0)
                scores(4)
                tiles(1)
                scores(5)
                if proj is not None:
                    pe.wait_ge(chl_ready, proj + 1)
                turn_att()
                tiles(2)
                scores(6)
                tiles(3)
                scores(7)
                products(0, 1)
                turn_maxima()
                products(2)
                values()
                if att is None:
                    products(3)
            else:
                scores(1, 2)
                if proj is not None:
                    if tail is not None:
                        pe.wait_ge(x.ao_ready, 4 * tail + 4)
                    turn_input()
                scores(3, 4)
                turn_att()
                if proj is not None:
                    pe.wait_ge(x.xhl_ready, proj + 1)
                tiles(0)
                scores(5)
                tiles(1)
                scores(6)
                tiles(2)
                scores(7)
                tiles(3)
                products(0, 1)
                turn_maxima()
                products(2, 3)
                values()
            if att is not None and y.cross:
                for b in range(G):
                    last = pe.matmul(y.bk[:, 2 + b // 2, (b % 2) * D:(b % 2 + 1) * D], sh.maskcT[:, :],
                                     y.vals[:, b, :, 0:HD], start=True, stop=True)
                    if b % 2:
                        last.then_inc(u_mm, 1)
            if att is not None:
                for qd in range(QUADS):
                    for n in range(4 * qd, 4 * qd + 4):
                        pe_shifted(pe, y, att, n)
                        if n == 3 and x.cross:
                            products(3)
                    if qd == 1:
                        if proj is not None:
                            pe.wait_ge(x.qk_lo, 4 * proj + 4)
                            pe.wait_ge(x.v_ready, 2 * proj + 2)
                    if qd == (2 if x.cross else 1) and tail is not None:
                        pe.wait_ge(x.op_out, tail + 1)
                    if qd > 0:
                        pe_values(pe, y, att, qd - 1)
                    if qd > 1:
                        pe_turn_outputs(pe, y, att, qd - 2)
                pe_values(pe, y, att, QUADS - 1)
                pe_turn_outputs(pe, y, att, QUADS - 2)
                pe.wait_ge(y.ao_ready, 4 * att + 2)

        with nc.Block() as block:
            @block.sync
            def _(sp):
                sp.dma_start(slf.src[:, :, :], x_groups[0]).then_inc(slf.loaded, 16)
                sp.dma_start(cin[:, :, :], ctx_groups[0]).then_inc(c_loaded, 16)
                sp.wait_ge(primed, 8)
                steps(sp, lambda *a: sp_slot(sp, *a))
                sp.wait_ge(stored, 16 * NG)

            @block.gpsimd
            def _(pool):
                for ch in (slf, crs):
                    nc.gpsimd.memset(ch.vals[:, :, :, :], 0.0).then_inc(primed, 1)
                    nc.gpsimd.memset(ch.stk[:, 1], 0.0).then_inc(primed, 1)
                for r in range(2):
                    pool.wait_ge(primed, 4 + 2 * r)
                    for ch in (slf, crs):
                        nc.gpsimd.affine_select(out=ch.stk[:, 1], in_=ch.stk[:, 1], compare_op=ALU.not_equal, fill=SHIFT,
                                                base=-(HALF * r + STACK + r), pattern=[[-2, FT // 2], [-FT, KT], [0, T]],
                                                channel_multiplier=1).then_inc(primed, 1)
                for ch in (slf, crs):
                    nc.gpsimd.memset(ch.vals[:, :, :, HD:HD + 1], WS).then_inc(primed, 1)
                steps(pool, lambda *a: pool_slot(pool, *a))

            @block.scalar
            def _(act):
                act.wait_ge(primed, 10)
                steps(act, act_slot)

            @block.vector
            def _(dve):
                steps(dve, dve_slot)

            @block.tensor
            def _(pe):
                steps(pe, pe_slot)


def ffn(nc, program, sh, x2_dram, out):
    x2_groups = x2_dram.rearrange("(n b) s d -> n s b d", b=G)
    out_groups = out.rearrange("(n b) s d -> n s b d", b=G)
    BODY = 2 * G
    HF = F // 2
    with ExitStack() as stack:
        sb, ps, sem = allocators(nc, stack, program)
        src = sb("ffn_src", [P, 2, G, D])
        stats = sb("ffn_stats", [P, G, 6])
        mv = sb("ffn_mv", [P, G, 2])
        ve = sb("ffn_ve", [P, G])
        rstd = sb("ffn_rstd", [P, G])
        nmr = sb("ffn_nmr", [P, G])
        xn = sb("ffn_xn", [P, G, D])
        xc = sb("ffn_xc", [P, 2, G, D])
        xhl = sb("ffn_xhl", [P, 2, 2, KT, 2 * S], F16)
        hid = sb("hid", [P, 2, F])
        hstats = sb("hstats", [P, 2, 2, 6])
        hmv = sb("hmv", [P, BODY, 2])
        hve = sb("hve", [P, BODY])
        hrstd = sb("hrstd", [P, BODY])
        cen = sb("cen", [P, 2, F])
        chl = sb("chl", [P, 2, 2, FT, S], F16)
        yn = sb("yn", [P, 2, D])
        y = sb("ffn_y", [P, 2, G, D])
        held = sb("ffn_held_wait", [P, 1])
        hbk = ps("hbk", [P, 2, 2, HF])
        cbk = ps("cbk", [P, 2, HF])
        xbk = ps("xbk", [P, KT, 2 * S])
        ybk = ps("ybk", [P, 512])
        loaded = [sem("even_loaded"), sem("odd_loaded")]
        stored = [sem("even_stored"), sem("odd_stored")]
        stats_done = sem("ffn_stats_done")
        moments, var_ready, rstd_ready = sem("ffn_moments"), sem("ffn_var_ready"), sem("ffn_rstd_ready")
        nmr_ready, xn_ready, xc_ready = sem("ffn_nmr_ready"), sem("ffn_xn_ready"), sem("ffn_xc_ready")
        xT_ready, xhi_ready, xlo_ready = sem("ffn_xT_ready"), sem("ffn_xhi_ready"), sem("ffn_xlo_ready")
        h_mm, hid_ready, hstats_done, hmv_ready = sem("h_mm"), sem("hid_ready"), sem("hstats_done"), sem("hmv_ready")
        hve_ready, hrstd_ready = sem("hve_ready"), sem("hrstd_ready")
        cen_ready, cenT_ready, chi_ready, clo_ready = sem("cen_ready"), sem("cenT_ready"), sem("cenhi_ready"), sem("cenlo_ready")
        y_mm, yn_ready, y_ready = sem("y_mm"), sem("yn_ready"), sem("ffn_y_ready")

        def here(k):
            return not isinstance(k, int) or 0 <= k < B

        def steps(engine, body):
            for i in (-1, 0):
                body(i)
            with engine.Fori(1, B // BODY - 2) as i:
                body(i)
            for i in range(B // BODY - 2, B // BODY + 1):
                body(i)

        def sp_body(sp, i):
            for half in range(2):
                s = 2 * i + half
                if here(4 * s - 4):
                    out_group = out_groups[s - 1]
                    sp.wait_ge(y_ready, 4 * s)
                    sp.dma_start(out_group, y[:, 1 - half]).then_inc(stored[1 - half], 16)
                if here(4 * s) and here(4 * s + 8):
                    x2_group = x2_groups[s + 2]
                    sp.wait_ge(xc_ready, s + 1)
                    sp.dma_start(src[:, half], x2_group).then_inc(loaded[half], 16)

        def pool_body(i):
            pool = nc.gpsimd
            for u in range(BODY):
                k, c = BODY * i + u, u % G
                half, n = 1 - u // G, 2 * i + u // G + 1
                if c == 0 and here(4 * n):
                    pool.wait_ge(moments, n + 1)
                    pool.tensor_tensor(ve[:, :], mv[:, :, 1], sh.eps[:, :], ALU.add).then_inc(var_ready, 1)
                    pool.wait_ge(var_ready, n + 1)
                    wait(pool, xn_ready, 2 * n)
                    pool.tensor_tensor(rstd[:, :], ve[:, :], sh.mhalf[:, :], ALU.pow).then_inc(rstd_ready, 1)
                if c == 0 and here(k):
                    pool.wait_ge(xn_ready, 2 * n)
                    wait(pool, y_ready, 4 * n - 8)
                    pool.tensor_tensor(xc[:, 1 - half], src[:, 1 - half], sh.c2B[:, :].unsqueeze(1).broadcast_to([P, G, D]),
                                       ALU.add).then_inc(xc_ready, 1)
                if here(k - 1):
                    v = (u - 1) % BODY
                    pool.wait_ge(hmv_ready, k)
                    pool.tensor_tensor(hve[:, v:v + 1], hmv[:, v, 1:2], sh.eps[:, 0:1], ALU.add).then_inc(hve_ready, 1)
                    pool.wait_ge(hve_ready, k)
                    pool.tensor_tensor(hrstd[:, v:v + 1], hve[:, v:v + 1], sh.mhalf[:, 0:1], ALU.pow).then_inc(hrstd_ready, 1)
                if here(k - 2):
                    h, b = (u - 2) % BODY // G, (u - 2) % G
                    if b == 0:
                        m = 2 * i + (u - 2) // G
                        pool.wait_ge(xc_ready, m + 1)
                        wait(pool, stored[h], 16 * (i + (u - 2) // BODY))
                    pool.wait_ge(yn_ready, k - 1)
                    pool.tensor_tensor(y[:, h, b], yn[:, u % 2], xc[:, h, b], ALU.add).then_inc(y_ready, 1)

        def act_body(i):
            act = nc.scalar
            for u in range(BODY):
                k, c, pair = BODY * i + u, u % G, BODY // 2 * i + u // 2
                n = 2 * i + u // G + 1
                if here(k):
                    act.wait_ge(h_mm, k + 1)
                    act.activation(hid[:, u % 2].rearrange("p (a h) -> p a h", a=2), hbk[:, u % 2], ACT.Gelu).then_inc(hid_ready, 1)
                if here(k - 1):
                    act.wait_ge(cenT_ready, k)
                    act.activation(chl[:, (u - 1) % 2, HI].rearrange("p (a t) s -> p a (t s)", a=2), cbk[:, :, :], ACT.Copy).then_inc(chi_ready, 1)
                if u % 2 == 0 and here(k + 2):
                    act.wait_ge(xT_ready, pair + 2)
                    act.activation(xhl[:, (u // 2 + 1) % 2, HI], xbk[:, :, :], ACT.Copy).then_inc(xhi_ready, 1)
                if here(k - 2):
                    v = (u - 2) % BODY
                    act.wait_ge(hrstd_ready, k - 1)
                    act.wait_ge(y_mm, k - 1)
                    wait(act, y_ready, k - 3)
                    act.activation(yn[:, u % 2], ybk[:, 0:D], ACT.Copy, scale=hrstd[:, v:v + 1]).then_inc(yn_ready, 1)
                if c % 2 and here(4 * n):
                    if c == 1:
                        act.wait_ge(nmr_ready, n + 1)
                    for b in (c - 1, c):
                        last = act.activation(xn[:, b], src[:, 1 - u // G, b], ACT.Identity, bias=nmr[:, b:b + 1], scale=rstd[:, b:b + 1])
                    last.then_inc(xn_ready, 1)

        def dve_body(i):
            dve = nc.vector
            for u in range(BODY):
                k, c, pair = BODY * i + u, u % G, BODY // 2 * i + u // 2
                half, n = 1 - u // G, 2 * i + u // G + 1
                if c == 0 and here(4 * n):
                    dve.wait_ge(stats_done, 4 * n + 4)
                    dve.memset(held[:, :], 0.0)
                    for b in range(G):
                        last = dve.bn_aggr(mv[:, b], stats[:, b])
                    last.then_inc(moments, 1)
                if c == 1 and here(4 * n):
                    dve.wait_ge(rstd_ready, n + 1)
                    dve.scalar_tensor_tensor(nmr[:, :], mv[:, :, 0], -1.0, rstd[:, :], ALU.mult, ALU.mult).then_inc(nmr_ready, 1)
                if here(k):
                    dve.wait_ge(hid_ready, k + 1)
                    for a in range(2):
                        last = dve.bn_stats(hstats[:, u % 2, a], hid[:, u % 2, a * HF:(a + 1) * HF])
                    last.then_inc(hstats_done, 1)
                    dve.wait_ge(hstats_done, k + 1)
                    dve.memset(held[:, :], 0.0)
                    dve.bn_aggr(hmv[:, u], hstats[:, u % 2].rearrange("p a s -> p (a s)")).then_inc(hmv_ready, 1)
                    dve.wait_ge(hmv_ready, k + 1)
                    dve.scalar_tensor_tensor(cen[:, u % 2], hid[:, u % 2], hmv[:, u, 0:1], sh.lnwB[:, :],
                                             ALU.subtract, ALU.mult).then_inc(cen_ready, 1)
                if here(k - 1):
                    dve.wait_ge(chi_ready, k)
                    dve.tensor_tensor(chl[:, (u - 1) % 2, LO].rearrange("p (a t) s -> p a (t s)", a=2), cbk[:, :, :],
                                      chl[:, (u - 1) % 2, HI].rearrange("p (a t) s -> p a (t s)", a=2), ALU.subtract).then_inc(clo_ready, 1)
                if u % 2 == 0 and here(k + 2):
                    dve.wait_ge(xhi_ready, pair + 2)
                    r = (u // 2 + 1) % 2
                    dve.tensor_tensor(xhl[:, r, LO], xbk[:, :, :], xhl[:, r, HI], ALU.subtract).then_inc(xlo_ready, 1)
                if c > 1 and here(4 * n + 4):
                    if c == 2:
                        dve.wait_ge(loaded[u // G], 16 * (i + 2))
                    for b in (2 * c - 4, 2 * c - 3):
                        dve.bn_stats(stats[:, b], src[:, u // G, b]).then_inc(stats_done, 1)

        def pe_body(i):
            pe = nc.tensor
            for u in range(BODY):
                k, pair = BODY * i + u, BODY // 2 * i + u // 2
                if here(k):
                    if u % 2 == 0:
                        pe.wait_ge(xlo_ready, pair + 1)
                    for a in range(2):
                        for part in (HI, LO):
                            for kt in range(KT):
                                last = pe.matmul(hbk[:, u % 2, a], xhl[:, u // 2 % 2, part, kt, u % 2 * S:(u % 2 + 1) * S],
                                                 sh.wfcT[:, kt, a * HF:(a + 1) * HF],
                                                 start=(part == HI and kt == 0), stop=(part == LO and kt == KT - 1))
                    last.then_inc(h_mm, 1)
                if here(k - 1):
                    pe.wait_ge(cen_ready, k)
                    wait(pe, clo_ready, k - 1)
                    for t in range(FT):
                        last = pe.transpose(cbk[:, t // 4, t % 4 * S:(t % 4 + 1) * S], cen[:, (u - 1) % 2, t * P:(t + 1) * P], sh.ident[:, :])
                    last.then_inc(cenT_ready, 1)
                if u % 2 == 0 and here(k + 2):
                    pe.wait_ge(xn_ready, pair + 2)
                    first = (u + 2) % G
                    for kt in range(KT):
                        for b in range(2):
                            last = pe.transpose(xbk[:, kt, b * S:(b + 1) * S], xn[:, first + b, kt * P:(kt + 1) * P], sh.ident[:, :])
                    last.then_inc(xT_ready, 1)
                if here(k - 2):
                    pe.wait_ge(clo_ready, k - 1)
                    wait(pe, yn_ready, k - 2)
                    for part in (HI, LO):
                        for t in range(FT):
                            last = pe.matmul(ybk[:, 0:D], chl[:, u % 2, part, t], sh.wpT[:, t],
                                             start=(part == HI and t == 0), stop=(part == LO and t == FT - 1))
                    last.then_inc(y_mm, 1)

        with nc.Block() as block:
            @block.sync
            def _(sp):
                for n in range(2):
                    sp.dma_start(src[:, n], x2_groups[n]).then_inc(loaded[n], 16)
                steps(sp, lambda i: sp_body(sp, i))
                for n in range(2):
                    sp.wait_ge(stored[n], 16 * (NG // 2))

            @block.gpsimd
            def _(pool):
                steps(pool, pool_body)

            @block.scalar
            def _(act):
                steps(act, act_body)

            @block.vector
            def _(dve):
                steps(dve, dve_body)

            @block.tensor
            def _(pe):
                steps(pe, pe_body)


INPUTS = ("x", "ctx_1024", "mask_1x1xSxS2_ik1",
          "L0_attn_Wq", "L0_attn_bq", "L0_attn_Wk", "L0_attn_bk", "L0_attn_Wv", "L0_attn_bv", "L0_attn_Wo", "L0_attn_bo",
          "L0_xattn_wq_w", "L0_xattn_wq_b", "L0_xattn_wk_w", "L0_xattn_wk_b", "L0_xattn_wv_w", "L0_xattn_wv_b",
          "L0_xattn_wo_w", "L0_xattn_wo_b", "L0_ffn_W_fc", "L0_ffn_ln_w", "L0_ffn_ln_b", "L0_ffn_W_proj")


def kernel(**inputs):
    import numpy as np
    import concourse.bacc as bacc
    from concourse.bass_utils import run_bass_kernel_spmd

    nc = bacc.Bacc("TRN2", target_bir_lowering=False, num_devices=1)
    arrays, aps = {}, []
    for name in INPUTS:
        a = np.ascontiguousarray(inputs[name])
        arrays["in_" + name] = a
        aps.append(nc.dram_tensor("in_" + name, a.shape, mybir.dt.from_np(a.dtype), kind="ExternalInput").ap())
    out = nc.dram_tensor("out_0", (B, S, D), F32, kind="ExternalOutput").ap()
    decoder_layer_kernel(nc, Inputs(*aps), out)
    result = run_bass_kernel_spmd(nc, [arrays], core_ids=[0])
    return result.results[0]["out_0"]
```
